# Optimizing a Trainium2 kernel written in Bass

```python
import numpy as np
import jax
import jax.numpy as jnp

def _softmax(x, axis=-1):
    return jax.nn.softmax(x, axis=axis)

def _gelu(x):
    return jax.nn.gelu(x, approximate=True)

def _silu(x):
    return jax.nn.silu(x)

def _sigmoid(x):
    return jax.nn.sigmoid(x)

def _layernorm(x, axis=-1, eps=1e-05):
    m = jnp.mean(x, axis=axis, keepdims=True)
    v = jnp.var(x, axis=axis, keepdims=True)
    return (x - m) / jnp.sqrt(v + eps)

def _scatter_add(tgt, idx, src, axis=0):
    return tgt.at[idx].add(src)

def _segment_sum(src, seg, n):
    return jax.ops.segment_sum(src, seg, n)
kernel_name = 'mk_prb_d1_jaxref_r8_8176f8'

def setup_inputs(seed: int=0):
    np.random.seed(seed)
    _w = jnp.asarray

    def _L0_attn_setup():
        import jax, jax.numpy as jnp
        import numpy as np
        B, S, D, H, DH = (4, 256, 128, 16, 64)
        SCALE = 1.0 / DH ** 0.5
        LN_EPS = 1e-05

        def _layer_norm(x, gamma, beta):
            mu = jnp.mean(x, axis=-1, keepdims=True)
            var = jnp.mean(jnp.square(x - mu), axis=-1, keepdims=True)
            return gamma * (x - mu) * jax.lax.rsqrt(var + LN_EPS) + beta
        key = jax.random.key(seed)
        ks = jax.random.split(key, 5)
        h = jax.random.normal(ks[0], (B, S, D), dtype=jnp.float32)
        Wq = SCALE * jax.random.normal(ks[1], (D, H * DH), dtype=jnp.float32)
        Wk = SCALE * jax.random.normal(ks[2], (D, H * DH), dtype=jnp.float32)
        Wv = SCALE * jax.random.normal(ks[3], (D, H * DH), dtype=jnp.float32)
        Wo = SCALE * jax.random.normal(ks[4], (H * DH, D), dtype=jnp.float32)
        gamma = jnp.ones((D,), dtype=jnp.float32)
        beta = jnp.zeros((D,), dtype=jnp.float32)
        return {'h': h, 'Wq': Wq, 'Wk': Wk, 'Wv': Wv, 'Wo': Wo, 'gamma': gamma, 'beta': beta}
    _L0_attn_in = _L0_attn_setup()

    def _L0_ffn_setup():
        import jax, jax.numpy as jnp
        import numpy as np
        D_MODEL, D_FF, N_EXPERTS, TOP_K = (128, 256, 8, 2)
        B, S = (2, 256)
        key = jax.random.key(seed)
        ks = jax.random.split(key, 6)
        sd = 1.0 / np.sqrt(D_MODEL)
        sf = 1.0 / np.sqrt(D_FF)
        return {'x': jax.random.normal(ks[0], (B, S, D_MODEL), jnp.float32), 'router_w': jax.random.normal(ks[1], (N_EXPERTS, D_MODEL), jnp.float32) * sd, 'gate_w': jax.random.normal(ks[2], (N_EXPERTS, D_MODEL, D_FF), jnp.float32) * sd, 'gate_b': jnp.zeros((N_EXPERTS, D_FF), jnp.float32), 'up_w': jax.random.normal(ks[3], (N_EXPERTS, D_MODEL, D_FF), jnp.float32) * sd, 'up_b': jnp.zeros((N_EXPERTS, D_FF), jnp.float32), 'down_w': jax.random.normal(ks[4], (N_EXPERTS, D_FF, D_MODEL), jnp.float32) * sf, 'down_b': jnp.zeros((N_EXPERTS, D_MODEL), jnp.float32)}
    _L0_ffn_in = _L0_ffn_setup()
    _d = {'L0_attn_h': _L0_attn_in['h'], 'L0_attn_Wq': _L0_attn_in['Wq'], 'L0_attn_Wk': _L0_attn_in['Wk'], 'L0_attn_Wv': _L0_attn_in['Wv'], 'L0_attn_Wo': _L0_attn_in['Wo'], 'L0_attn_gamma': _L0_attn_in['gamma'], 'L0_attn_beta': _L0_attn_in['beta'], 'L0_ffn_router_w': _L0_ffn_in['router_w'], 'L0_ffn_gate_w': _L0_ffn_in['gate_w'], 'L0_ffn_gate_b': _L0_ffn_in['gate_b'], 'L0_ffn_up_w': _L0_ffn_in['up_w'], 'L0_ffn_up_b': _L0_ffn_in['up_b'], 'L0_ffn_down_w': _L0_ffn_in['down_w'], 'L0_ffn_down_b': _L0_ffn_in['down_b']}
    _x0 = _d['L0_attn_h']
    _d['L0_attn_h'] = jax.random.normal(jax.random.fold_in(jax.random.key(seed), 1), (4, 512, 128), dtype=_x0.dtype)
    del _x0
    return _d

def reference(L0_attn_h, L0_attn_Wq, L0_attn_Wk, L0_attn_Wv, L0_attn_Wo, L0_attn_gamma, L0_attn_beta, L0_ffn_router_w, L0_ffn_gate_w, L0_ffn_gate_b, L0_ffn_up_w, L0_ffn_up_b, L0_ffn_down_w, L0_ffn_down_b):

    def _L0_attn_ref(h, Wq, Wk, Wv, Wo, gamma, beta):
        import jax, jax.numpy as jnp
        import numpy as np
        B, S, D, H, DH = (4, 256, 128, 16, 64)
        SCALE = 1.0 / DH ** 0.5
        LN_EPS = 1e-05

        def _layer_norm(x, gamma, beta):
            mu = jnp.mean(x, axis=-1, keepdims=True)
            var = jnp.mean(jnp.square(x - mu), axis=-1, keepdims=True)
            return gamma * (x - mu) * jax.lax.rsqrt(var + LN_EPS) + beta
        b, s, d = h.shape
        q = (h @ Wq).reshape(b, s, H, DH)
        k = (h @ Wk).reshape(b, s, H, DH)
        v = (h @ Wv).reshape(b, s, H, DH)
        scores = jnp.einsum('bind,bjnd->bijn', q, k) * SCALE
        probs = jax.nn.softmax(scores, axis=2)
        attn_vec = jnp.einsum('bijn,bjnd->bind', probs, v).reshape(b, s, H * DH)
        attn_out = attn_vec @ Wo
        return _layer_norm(h + attn_out, gamma, beta)

    def _L0_ffn_ref(x, router_w, gate_w, gate_b, up_w, up_b, down_w, down_b):
        import jax, jax.numpy as jnp
        import numpy as np
        D_MODEL, D_FF, N_EXPERTS, TOP_K = (128, 256, 8, 2)
        B, S = (2, 256)
        b, s, d = x.shape
        xf = x.reshape(b * s, d)
        n = xf.shape[0]
        router_logits = xf @ router_w.T
        probs = jax.nn.softmax(router_logits, axis=-1)
        topv, topi = jax.lax.top_k(probs, TOP_K)
        mask = jnp.zeros_like(probs).at[jnp.arange(n)[:, None], topi].set(1.0)
        probs = probs * mask
        probs = probs / (probs.sum(axis=-1, keepdims=True) + 1e-09)
        g = jnp.einsum('nd,edf->nef', xf, gate_w) + gate_b
        u = jnp.einsum('nd,edf->nef', xf, up_w) + up_b
        h = jax.nn.silu(g) * u
        expert_out = jnp.einsum('nef,efd->ned', h, down_w) + down_b
        y = jnp.einsum('ne,ned->nd', probs, expert_out)
        return y.reshape(b, s, d)
    x = L0_attn_h
    xn = _layernorm(x, axis=-1)
    x = x + _L0_attn_ref(xn, L0_attn_Wq, L0_attn_Wk, L0_attn_Wv, L0_attn_Wo, L0_attn_gamma, L0_attn_beta) + _L0_ffn_ref(xn, L0_ffn_router_w, L0_ffn_gate_w, L0_ffn_gate_b, L0_ffn_up_w, L0_ffn_up_b, L0_ffn_down_w, L0_ffn_down_b)
    return x

_drawn_inputs = setup_inputs


def setup_inputs(seed=0):
    import zlib

    import numpy as np

    out = dict(_drawn_inputs(seed))
    spreads = {'L0_attn_gamma': (1.0, 0.2),
     'L0_attn_beta': (0.0, 0.1),
     'L0_ffn_gate_b': (0.0, 0.339),
     'L0_ffn_up_b': (0.0, 0.336),
     'L0_ffn_down_b': (0.0, 0.1)}
    factors = {}
    for name, (base, spread) in spreads.items():
        noise = np.random.default_rng([zlib.crc32(name.encode()), seed]).standard_normal(out[name].shape)
        drawn = base * np.exp(spread * noise) if base else spread * noise
        out[name] = jnp.asarray(drawn.astype(out[name].dtype))
    for name, factor in factors.items():
        out[name] = (out[name] * factor).astype(out[name].dtype)
    return out
```

```python
from contextlib import ExitStack

import concourse.bass as bass
from concourse import mybir

ALU = mybir.AluOpType
ACT = mybir.ActivationFunctionType
AX = mybir.AxisListType
F32 = mybir.dt.float32
F32R = mybir.dt.float32r

P = 128
B, S, D = 4, 512, 128
T = B * S
NT = T // P
TB = S // P
DH = 64
NP = 8
E = 8
F = 256
NF = F // P
EPS = 1e-5
SCALE = DH ** -0.5


def layer_kernel(nc: bass.Bass, x, wq, wk, wv, wo, gamma, beta, router_w,
                 gate_w, gate_b, up_w, up_b, down_w, down_b, out):
    xr = x.rearrange("b (t p) d -> p (b t) d", p=P)
    outr = out.rearrange("b (t p) d -> p (b t) d", p=P)

    with ExitStack() as ctx:
        def sb(stack, name, shape, dt=F32):
            return stack.enter_context(nc.sbuf_tensor(name, shape, dt))

        def sem(name):
            return ctx.enter_context(nc.semaphore(name))

        ident = sb(ctx, "ident", [P, P])
        ones = sb(ctx, "ones", [P, P])
        x_in = sb(ctx, "x_in", [P, NT, D])
        xn = sb(ctx, "xn", [P, NT, D])
        xt = sb(ctx, "xt", [P, T])
        xt_hi = sb(ctx, "xt_hi", [P, T], F32R)
        xt_lo = sb(ctx, "xt_lo", [P, T], F32R)
        gb = sb(ctx, "gb", [P, 2, D])
        rwt = sb(ctx, "rwt", [P, E])
        biast = sb(ctx, "biast", [P, 2, E * NF])
        down_bias = sb(ctx, "down_bias", [E, D])
        small = sb(ctx, "small", [P, 8, NT])

        psum = ctx.enter_context(nc.psum_tensor("psum", [P, 8, 512], F32))

        prepare_phase(nc, ctx, sb, sem, psum, ident, ones, x_in, xn, xt, xt_hi, xt_lo, gb, rwt, biast,
                      down_bias, small, xr, wq, wk, wv, wo, gamma, beta, router_w, gate_b, up_b, down_b)
        experts_phase(nc, sb, sem, psum, ident, ones, x_in, xn, xt, xt_hi, xt_lo, gb, rwt, biast, down_bias,
                      small, gate_w, up_w, down_w, outr)


def prepare_phase(nc, ctx, sb, sem, psum, ident, ones, x_in, xn, xt, xt_hi, xt_lo, gb, rwt, biast,
                  down_bias, small, xr, wq, wk, wv, wo, gamma, beta, router_w, gate_b, up_b, down_b):
    with ExitStack() as att:
        wqk = sb(att, "wqk", [P, 2, NP * P])
        wo_sb = sb(att, "wo_sb", [P, NP, D])
        v_all = sb(att, "v_all", [P, NT, NP * P])
        wqk_hi = sb(att, "wqk_hi", [P, 2, P], F32R)
        wqk_lo = sb(att, "wqk_lo", [P, 2, P], F32R)

        x_loaded = [sem(f"x_loaded{b}") for b in range(B)]
        wv_loaded = sem("wv_loaded")
        rows_loaded = sem("rows_loaded")
        weights_loaded = sem("weights_loaded")
        const_made = sem("const_made")
        wv_split = sem("wv_split")
        stat_step = sem("stat_step")
        var_ready = sem("var_ready")
        root_ready = sem("root_ready")
        xn_ready = sem("xn_ready")
        xt_turned = sem("xt_turned")
        xt_copied = sem("xt_copied")
        xt_hi_ready = sem("xt_hi_ready")
        xt_lo_ready = sem("xt_lo_ready")
        rows_turned = sem("rows_turned")
        rows_kept = sem("rows_kept")
        v_ready = sem("v_ready")
        v_kept_act = sem("v_kept_act")
        v_kept_dve = sem("v_kept_dve")
        w_split = sem("w_split")

        with ExitStack() as prep:
            wv_in = sb(prep, "wv_in", [P, NP * P])
            wv_hi = sb(prep, "wv_hi", [P, NP * P], F32R)
            wv_lo = sb(prep, "wv_lo", [P, NP * P], F32R)
            rows = sb(prep, "rows", [P, 3, D])
            grow = sb(prep, "grow", [1, 2, D])
            stats = sb(prep, "stats", [P, NT, 6])
            mv = sb(prep, "mv", [P, NT, 2])
            block = prep.enter_context(nc.Block())
            bank_x, bank_v = 0, 4
            bias_rows, router_rows = rows[0:2 * E * NF, 0, :], rows[0:E, 1, :]

            @block.sync
            def _(sp):
                for b in range(B):
                    sp.dma_start(x_in[:, TB * b:TB * b + TB, :], xr[:, TB * b:TB * b + TB, :])\
                      .then_inc(x_loaded[b], 16)
                sp.dma_start(wv_in[:, :], wv).then_inc(wv_loaded, 16)
                sp.dma_start(wqk[:, 0, :], wq).then_inc(weights_loaded, 16)
                sp.dma_start(wqk[:, 1, :], wk).then_inc(weights_loaded, 16)
                sp.dma_start(wo_sb[:, :, :], wo.rearrange("(n f) d -> f n d", f=P)).then_inc(weights_loaded, 16)

            @block.gpsimd
            def _(pool):
                pool.memset(ident[:, :], 0.0).then_inc(const_made, 1)
                pool.memset(ones[:, :], 1.0).then_inc(const_made, 1)
                pool.wait_ge(const_made, 2)
                pool.affine_select(out=ident[:, :], in_=ident[:, :], compare_op=ALU.not_equal, fill=1.0,
                                   base=0, pattern=[[-1, P]], channel_multiplier=1).then_inc(const_made, 1)
                pool.wait_ge(wv_loaded, 16)
                pool.tensor_copy(wv_hi[:, :], wv_in[:, :]).then_inc(wv_split, 1)
                pool.wait_ge(wv_split, 1)
                pool.tensor_tensor(wv_lo[:, :], wv_in[:, :], wv_hi[:, :].bitcast(F32), ALU.subtract)\
                    .then_inc(wv_split, 1)

            @block.scalar
            def _(act):
                act.dma_start(rows[0:E * NF, 0, :], gate_b.rearrange("e (c p) -> (e c) p", p=P))\
                   .then_inc(rows_loaded, 16)
                act.dma_start(rows[E * NF:2 * E * NF, 0, :], up_b.rearrange("e (c p) -> (e c) p", p=P))\
                   .then_inc(rows_loaded, 16)
                act.dma_start(router_rows, router_w).then_inc(rows_loaded, 16)
                act.dma_start(grow[:, 0, :], gamma.rearrange("(a n) -> a n", a=1)).then_inc(rows_loaded, 16)
                act.dma_start(grow[:, 1, :], beta.rearrange("(a n) -> a n", a=1)).then_inc(rows_loaded, 16)
                act.dma_start(down_bias[:, :], down_b).then_inc(rows_loaded, 16)
                for b in range(B):
                    act.wait_ge(var_ready, b + 1)
                    act.activation(small[:, 1, TB * b:TB * b + TB], small[:, 0, TB * b:TB * b + TB], ACT.Sqrt)\
                       .then_inc(root_ready, 1)
                for b in range(B):
                    act.wait_ge(xt_turned, b + 1)
                    act.activation(xt_hi[:, S * b:S * b + S], psum[:, bank_x + b, :], ACT.Copy)\
                       .then_inc(xt_hi_ready, 1)
                    act.activation(xt[:, S * b:S * b + S], psum[:, bank_x + b, :], ACT.Copy)\
                       .then_inc(xt_copied, 1)
                for t in range(NT):
                    act.wait_ge(v_ready, 2 * t + 1)
                    act.activation(v_all[:, t, 0:512], psum[:, bank_v + 2 * (t % 2), :], ACT.Copy)\
                       .then_inc(v_kept_act, 1)

            @block.vector
            def _(dve):
                step = 0
                for b in range(B):
                    g = slice(TB * b, TB * b + TB)
                    dve.wait_ge(x_loaded[b], 16)
                    for t in range(TB * b, TB * b + TB):
                        dve.bn_stats(stats[:, t, :], x_in[:, t, :]).then_inc(stat_step, 1)
                    step += TB
                    dve.wait_ge(stat_step, step)
                    for t in range(TB * b, TB * b + TB):
                        dve.bn_aggr(mv[:, t, :], stats[:, t, :]).then_inc(stat_step, 1)
                    step += TB
                    dve.wait_ge(stat_step, step)
                    dve.tensor_scalar(small[:, 0, g], mv[:, g, 1], EPS, None, ALU.add).then_inc(var_ready, 1)
                for b in range(B):
                    g = slice(TB * b, TB * b + TB)
                    dve.wait_ge(root_ready, b + 1)
                    step = reciprocal_root(dve, small, g, stat_step, step)
                    for t in range(TB * b, TB * b + TB):
                        dve.tensor_scalar(xn[:, t, :], x_in[:, t, :], mv[:, t, 0:1], small[:, 2, t:t + 1],
                                          ALU.subtract, ALU.mult).then_inc(xn_ready, 1)
                dve.wait_ge(weights_loaded, 48)
                dve.tensor_copy(wqk_hi[:, :, :], wqk[:, :, 0:P]).then_inc(w_split, 1)
                dve.wait_ge(w_split, 1)
                dve.tensor_tensor(wqk_lo[:, :, :], wqk[:, :, 0:P], wqk_hi[:, :, :].bitcast(F32), ALU.subtract)\
                   .then_inc(w_split, 1)
                for b in range(B):
                    dve.wait_ge(xt_hi_ready, b + 1)
                    dve.wait_ge(xt_copied, b + 1)
                    dve.tensor_tensor(xt_lo[:, S * b:S * b + S], psum[:, bank_x + b, :],
                                      xt_hi[:, S * b:S * b + S].bitcast(F32), ALU.subtract)\
                       .then_inc(xt_lo_ready, 1)
                dve.wait_ge(rows_turned, 1)
                dve.tensor_copy(biast[:, :, :].rearrange("p a n -> p (a n)"), psum[:, bank_x, 0:2 * E * NF])\
                   .then_inc(rows_kept, 1)
                dve.tensor_copy(rwt[:, :], psum[:, bank_x, 64:64 + E]).then_inc(rows_kept, 1)
                dve.tensor_copy(gb[:, :, :].rearrange("p a n -> p (a n)"), psum[:, bank_x, 128:128 + 2 * D])\
                   .then_inc(rows_kept, 1)
                for t in range(NT):
                    dve.wait_ge(v_ready, 2 * t + 2)
                    dve.tensor_copy(v_all[:, t, 512:1024], psum[:, bank_v + 1 + 2 * (t % 2), :])\
                       .then_inc(v_kept_dve, 1)

            @block.tensor
            def _(pe):
                pe.wait_ge(const_made, 3)
                for b in range(B):
                    for k in range(TB):
                        pe.wait_ge(xn_ready, TB * b + k + 1)
                        mm = pe.transpose(psum[:, bank_x + b, P * k:P * k + P], xn[:, TB * b + k, :], ident[:, :])
                    mm.then_inc(xt_turned, 1)
                pe.wait_ge(rows_loaded, 96)
                pe.wait_ge(xt_lo_ready, 1)
                n = 2 * E * NF
                pe.transpose(psum[:, bank_x, 0:n], bias_rows, ident[0:n, 0:n])
                pe.transpose(psum[:, bank_x, 64:64 + E], router_rows, ident[0:E, 0:E])
                for a in range(2):
                    mm = pe.matmul(psum[:, bank_x, 128 + D * a:128 + D * a + D], ones[0:1, :], grow[:, a, :],
                                   start=True, stop=True)
                mm.then_inc(rows_turned, 1)
                pe.wait_ge(wv_split, 2)
                for t in range(NT):
                    pe.wait_ge(xt_lo_ready, t // TB + 1)
                    for half in range(2):
                        if t >= 2:
                            pe.wait_ge((v_kept_act, v_kept_dve)[half], t - 1)
                        bank = psum[:, bank_v + half + 2 * (t % 2), :]
                        cols, tok = slice(512 * half, 512 * half + 512), slice(P * t, P * t + P)
                        pe.matmul(bank, xt_hi[:, tok], wv_hi[:, cols], start=True, stop=False)
                        pe.matmul(bank, xt_hi[:, tok], wv_lo[:, cols], start=False, stop=False)
                        pe.matmul(bank, xt_lo[:, tok], wv_hi[:, cols], start=False, stop=True).then_inc(v_ready, 1)

        attention_phase(nc, att, sb, sem, psum, ident, ones, xn, xt_hi, xt_lo, wqk, wo_sb, v_all,
                        wqk_hi, wqk_lo, w_split)


def reciprocal_root(dve, small, g, stat_step, step):
    dve.reciprocal(small[:, 2, g], small[:, 1, g]).then_inc(stat_step, 1)
    dve.wait_ge(stat_step, step + 1)
    dve.tensor_tensor(small[:, 3, g], small[:, 2, g], small[:, 2, g], ALU.mult).then_inc(stat_step, 1)
    dve.wait_ge(stat_step, step + 2)
    dve.tensor_tensor(small[:, 3, g], small[:, 3, g], small[:, 0, g], ALU.mult).then_inc(stat_step, 1)
    dve.wait_ge(stat_step, step + 3)
    dve.tensor_scalar(small[:, 3, g], small[:, 3, g], -0.5, 1.5, ALU.mult, ALU.add).then_inc(stat_step, 1)
    dve.wait_ge(stat_step, step + 4)
    dve.tensor_tensor(small[:, 2, g], small[:, 2, g], small[:, 3, g], ALU.mult).then_inc(stat_step, 1)
    dve.wait_ge(stat_step, step + 5)
    return step + 5


def attention_phase(nc, att, sb, sem, psum, ident, ones, xn, xt_hi, xt_lo, wqk, wo_sb, v_all,
                    wqk_hi, wqk_lo, w_split):
    k_stack = sb(att, "k_stack", [P, 2, 2, S], F32R)
    q_stack = sb(att, "q_stack", [P, 2, 2, S], F32R)
    k_ones = sb(att, "k_ones", [DH + 2, 2, 2, S], F32R)
    q_max = sb(att, "q_max", [DH + 2, 2, 2, S], F32R)
    v_pair = sb(att, "v_pair", [P, 2, TB, P])
    probs = sb(att, "probs", [P, 2, TB, 2, S])
    psums = sb(att, "psums", [P, 2, 2, S])
    o_norm = sb(att, "o_norm", [P, 2, S])
    inv_den = sb(att, "inv_den", [P, S])
    o_raw = sb(att, "o_raw", [P, S])
    q_top = sb(att, "q_top", [P, 2, 2 * TB])
    neg = sb(att, "neg", [2 * TB, 2, 2, P], F32R)

    sc_bank, mx_bank = 0, 4
    q_bank, k_bank = mx_bank, mx_bank + 1
    o_psum = psum[:, 6, :]
    den_psum = psum[:, 7, :]

    ones_set = sem("ones_set")
    qk_ready = sem("qk_ready")
    hi_ready = sem("hi_ready")
    copied = [sem(f"copied{par}") for par in range(2)]
    o_copied = sem("o_copied")
    lo_ready = sem("lo_ready")
    top_scores = sem("top_scores")
    top_ready = sem("top_ready")
    top_turned = sem("top_turned")
    neg_ready = sem("neg_ready")
    max_rows = sem("max_rows")
    scores_ready = sem("scores_ready")
    probs_ready = sem("probs_ready")
    v_copied = sem("v_copied")
    part_sums = sem("part_sums")
    sums_ready = sem("sums_ready")
    pv_done = sem("pv_done")
    den_ready = sem("den_ready")
    inv_ready = sem("inv_ready")
    o_ready = sem("o_ready")
    wo_ready = sem("wo_ready")
    added = sem("added")

    LAST = NP * B - 1

    def walk(eng, unit):
        for b in range(B):
            unit(0, b, b == 0, 2)
        with eng.Fori(1, NP - 1) as pair:
            for b in range(B):
                unit(pair, b, False, 2)
        for b in range(B):
            unit(NP - 1, b, False, min(2, B - 1 - b))

    def following(pair, b, by=1):
        return (pair, b + by) if b + by < B else (pair + 1, b + by - B)

    def preceding(pair, b):
        return (pair, b - 1) if b else (pair - 1, B - 1)

    with ExitStack() as run:
        block = run.enter_context(nc.Block())

        @block.tensor
        def _(pe):
            def project(pair, b):
                u, tok = 4 * pair + b, slice(S * b, S * b + S)
                pe.wait_ge(w_split, 2 * (pair + 1))
                for which, bank in ((1, k_bank), (0, q_bank)):
                    o = psum[:, bank, :]
                    pe.matmul(o, wqk_hi[:, which, :], xt_hi[:, tok], start=True, stop=False)
                    pe.matmul(o, wqk_lo[:, which, :], xt_hi[:, tok], start=False, stop=False)
                    pe.matmul(o, wqk_hi[:, which, :], xt_lo[:, tok], start=False, stop=True).then_inc(qk_ready, 1)

            def scores_for_max(pair, b, js):
                u, par = 4 * pair + b, b % 2
                for j in js:
                    h, qt = j // TB, j % TB
                    if j == 0:
                        pe.wait_ge(hi_ready, 4 * u + 4)
                        pe.wait_ge(lo_ready, 4 * u + 4)
                    if j >= 2:
                        pe.wait_ge(top_ready, 8 * u + j - 1)
                    pe.matmul(psum[:, mx_bank + j % 2, :], q_stack[0:DH, par, h, P * qt:P * qt + P],
                              k_ones[0:DH, par, h, :], start=True, stop=True).then_inc(top_scores, 1)

            def turn_max(pair, b):
                u, par = 4 * pair + b, b % 2
                pe.wait_ge(top_ready, 8 * u + 8)
                pe.transpose(den_psum[0:2 * TB, 0:P], q_top[:, par, :], ident[:, :]).then_inc(top_turned, 1)

            def scores_stacked(u, par, kt):
                if kt == 0:
                    pe.wait_ge(copied[par], 16 * (u - par) + 32)
                for h in range(2):
                    pe.matmul(psum[:, sc_bank + 2 * (kt % 2) + h, :], k_stack[:, par, h, P * kt:P * kt + P],
                              q_stack[:, par, h, :], start=True, stop=False)

            def scores_rest(u, par, kt):
                for h in range(2):
                    mm = pe.matmul(psum[:, sc_bank + 2 * (kt % 2) + h, :], k_ones[:, par, h, P * kt:P * kt + P],
                                   q_max[:, par, h, :], start=False, stop=True)
                mm.then_inc(scores_ready, 1)

            def values(u, par, kt):
                for h in range(2):
                    mm = pe.matmul(o_psum[DH * h:DH * h + DH, :], v_pair[:, par, kt, DH * h:DH * h + DH],
                                   probs[:, par, kt, h, :], start=(kt == 0), stop=(kt == TB - 1))
                if kt == TB - 1:
                    mm.then_inc(pv_done, 1)

            def denominators(u):
                pe.wait_ge(sums_ready, u + 1)
                for h in range(2):
                    mm = pe.matmul(den_psum[DH * h:DH * h + DH, :], ones[:, 0:DH], psums[:, 0, h, :],
                                   start=True, stop=True)
                mm.then_inc(den_ready, 1)

            def output_share(pair, b):
                u, par = 4 * pair + b, b % 2
                pe.wait_ge(o_ready, u + 1)
                for t in range(TB):
                    mm = pe.matmul(den_psum[:, P * t:P * t + P], o_norm[:, par, P * t:P * t + P],
                                   wo_sb[:, pair, :], start=True, stop=True)
                mm.then_inc(wo_ready, 1)

            def unit(pair, b, first, left):
                u, par = 4 * pair + b, b % 2
                if not first:
                    pe.wait_ge(probs_ready, 4 * u - 1)
                scores_stacked(u, par, 0)
                if not first:
                    pe.wait_ge(probs_ready, 4 * u)
                scores_stacked(u, par, 1)
                if not first:
                    pe.wait_ge(neg_ready, 2 * u + 2)
                    denominators(u - 1)
                pe.wait_ge(max_rows, 32 * u + 32)
                scores_rest(u, par, 0)
                scores_rest(u, par, 1)
                pe.wait_ge(probs_ready, 4 * u + 1)
                scores_stacked(u, par, 2)
                scores_rest(u, par, 2)
                if not first:
                    pe.wait_ge(o_copied, u)
                pe.wait_ge(v_copied, u + 1)
                values(u, par, 0)
                if left:
                    scores_for_max(*following(pair, b), range(0, 2))
                pe.wait_ge(probs_ready, 4 * u + 2)
                scores_stacked(u, par, 3)
                scores_rest(u, par, 3)
                if left:
                    scores_for_max(*following(pair, b), range(2, 4))
                if not first:
                    output_share(*preceding(pair, b))
                if left:
                    scores_for_max(*following(pair, b), range(4, 6))
                values(u, par, 1)
                if left:
                    scores_for_max(*following(pair, b), range(6, 8))
                pe.wait_ge(probs_ready, 4 * u + 3)
                values(u, par, 2)
                if left:
                    if not first:
                        pe.wait_ge(added, u)
                    turn_max(*following(pair, b))
                if left > 1:
                    pe.wait_ge(top_ready, 8 * u + 16)
                    project(*following(pair, b, 2))
                pe.wait_ge(probs_ready, 4 * u + 4)
                values(u, par, 3)

            project(0, 0)
            scores_for_max(0, 0, range(8))
            turn_max(0, 0)
            pe.wait_ge(top_ready, 8)
            project(0, 1)
            walk(pe, unit)
            pe.wait_ge(added, LAST)
            denominators(LAST)
            output_share(NP - 1, B - 1)

        @block.scalar
        def _(act):
            def upper(pair, b):
                u, par = 4 * pair + b, b % 2
                act.wait_ge(qk_ready, 2 * u + 1)
                for h in range(2):
                    act.activation(k_ones[0:DH, par, h, :], psum[DH * h:DH * h + DH, k_bank, :], ACT.Copy)\
                       .then_inc(hi_ready, 1)
                act.wait_ge(qk_ready, 2 * u + 2)
                for h in range(2):
                    act.activation(q_stack[0:DH, par, h, :], psum[DH * h:DH * h + DH, q_bank, :], ACT.Copy)\
                       .then_inc(hi_ready, 1)

            def copy_output(u):
                act.wait_ge(pv_done, u + 1)
                act.activation(o_raw[:, :], o_psum, ACT.Copy).then_inc(o_copied, 1)

            def exponent(u, par, kt):
                act.wait_ge(scores_ready, 4 * u + kt + 1)
                act.activation(probs[:, par, kt, :, :], psum[:, sc_bank + 2 * (kt % 2):sc_bank + 2 * (kt % 2) + 2, :],
                               ACT.Exp, scale=SCALE).then_inc(probs_ready, 1)

            def unit(pair, b, first, left):
                u, par = 4 * pair + b, b % 2
                if not isinstance(pair, int) or u >= 2:
                    act.wait_ge(pv_done, u - 1)
                    act.wait_ge(sums_ready, u - 1)
                for kt in range(TB):
                    exponent(u, par, kt)
                if left > 1:
                    upper(*following(pair, b, 2))
                if not first:
                    act.wait_ge(o_ready, u)
                copy_output(u)

            upper(0, 0)
            upper(0, 1)
            walk(act, unit)

        @block.vector
        def _(dve):
            def lower(pair, b):
                u, par = 4 * pair + b, b % 2
                dve.wait_ge(hi_ready, 4 * u + 2)
                for h in range(2):
                    dve.tensor_tensor(k_stack[DH:P, par, h, :], psum[DH * h:DH * h + DH, k_bank, :],
                                      k_ones[0:DH, par, h, :].bitcast(F32), ALU.subtract).then_inc(lo_ready, 1)
                dve.wait_ge(hi_ready, 4 * u + 4)
                for h in range(2):
                    dve.tensor_tensor(q_max[0:DH, par, h, :], psum[DH * h:DH * h + DH, q_bank, :],
                                      q_stack[0:DH, par, h, :].bitcast(F32), ALU.subtract).then_inc(lo_ready, 1)

            def maxima(pair, b, js):
                u, par = 4 * pair + b, b % 2
                for j in js:
                    dve.wait_ge(top_scores, 8 * u + j + 1)
                    dve.tensor_reduce(q_top[:, par, j:j + 1], psum[:, mx_bank + j % 2, :], AX.X, ALU.max)\
                       .then_inc(top_ready, 1)

            def negate(pair, b):
                u, par = 4 * pair + b, b % 2
                turned = den_psum[0:2 * TB, 0:P]
                dve.wait_ge(top_turned, u + 1)
                dve.tensor_scalar(neg[:, par, 0, :], turned, -1.0, None, ALU.mult).then_inc(neg_ready, 1)
                dve.wait_ge(neg_ready, 2 * u + 1)
                dve.scalar_tensor_tensor(out=neg[:, par, 1, :], in0=turned, scalar=-1.0,
                                         in1=neg[:, par, 0, :].bitcast(F32), op0=ALU.mult, op1=ALU.subtract)\
                   .then_inc(neg_ready, 1)

            def normalise(pair, b):
                u, par = 4 * pair + b, b % 2
                dve.wait_ge(den_ready, u + 1)
                dve.reciprocal(inv_den[:, :], den_psum).then_inc(inv_ready, 1)
                dve.wait_ge(inv_ready, u + 1)
                dve.wait_ge(o_copied, u + 1)
                dve.tensor_tensor(o_norm[:, par, :], o_raw[:, :], inv_den[:, :], ALU.mult).then_inc(o_ready, 1)

            def add_share(pair, b):
                u = 4 * pair + b
                dve.wait_ge(wo_ready, u + 1)
                share = xn[:, TB * b:TB * b + TB, :].rearrange("p t d -> p (t d)")
                if not isinstance(pair, int) or u:
                    dve.wait_ge(added, u)
                dve.tensor_tensor(share, den_psum, share, ALU.add).then_inc(added, 1)

            def split_weights(pair, u):
                dve.wait_ge(qk_ready, 2 * u + 2)
                src = wqk[:, :, bass.ds(pair * P, P)]
                dve.tensor_copy(wqk_hi[:, :, :], src).then_inc(w_split, 1)
                dve.wait_ge(w_split, 2 * pair + 1)
                dve.tensor_tensor(wqk_lo[:, :, :], src, wqk_hi[:, :, :].bitcast(F32), ALU.subtract)\
                   .then_inc(w_split, 1)

            def unit(pair, b, first, left):
                u = 4 * pair + b
                if not first:
                    normalise(*preceding(pair, b))
                if left:
                    maxima(*following(pair, b), range(0, 6))
                if not first:
                    add_share(*preceding(pair, b))
                if left:
                    maxima(*following(pair, b), range(6, 8))
                    negate(*following(pair, b))
                if left > 1:
                    lower(*following(pair, b, 2))
                if b == 1 and not (isinstance(pair, int) and pair == NP - 1):
                    split_weights(pair + 1, u + 2)

            dve.memset(k_ones[DH:DH + 2, :, :, :].rearrange("r a h s -> r (a h s)").bitcast(F32), 1.0)\
               .then_inc(ones_set, 1)
            lower(0, 0)
            maxima(0, 0, range(8))
            dve.wait_ge(ones_set, 1)
            negate(0, 0)
            lower(0, 1)
            walk(dve, unit)
            normalise(NP - 1, B - 1)
            add_share(NP - 1, B - 1)

        @block.gpsimd
        def _(pool):
            def copy_v(pair, b):
                pool.tensor_copy(v_pair[:, b % 2, :, :], v_all[:, TB * b:TB * b + TB, bass.ds(pair * P, P)])\
                    .then_inc(v_copied, 1)

            def unit(pair, b, first, left):
                u, par = 4 * pair + b, b % 2
                later = not isinstance(pair, int)
                pool.wait_ge(probs_ready, 4 * u + 2)
                if later or u:
                    pool.wait_ge(sums_ready, u)
                    pool.wait_ge(den_ready, u)
                pool.tensor_tensor(psums[:, 0, :, :], probs[:, par, 0, :, :], probs[:, par, 1, :, :], ALU.add)\
                    .then_inc(part_sums, 1)
                if left:
                    if later or u:
                        pool.wait_ge(pv_done, u)
                    copy_v(*following(pair, b))
                pool.wait_ge(probs_ready, 4 * u + 4)
                pool.tensor_tensor(psums[:, 1, :, :], probs[:, par, 2, :, :], probs[:, par, 3, :, :], ALU.add)\
                    .then_inc(part_sums, 1)
                pool.wait_ge(part_sums, 2 * u + 2)
                pool.tensor_tensor(psums[:, 0, :, :], psums[:, 0, :, :], psums[:, 1, :, :], ALU.add)\
                    .then_inc(sums_ready, 1)

            copy_v(0, 0)
            walk(pool, unit)

        @block.sync
        def _(sp):
            def move_max(pair, b):
                u, par = 4 * pair + b, b % 2
                for part in range(2):
                    sp.wait_ge(neg_ready, 2 * u + part + 1)
                    row = q_max[DH + part:DH + part + 1, par, :, :].rearrange("r h (t q) -> r (h t) q", q=P)
                    sp.dma_start(row.bitcast(F32), neg[:, par, part, :].bitcast(F32)).then_inc(max_rows, 16)

            def copy_upper(pair, b):
                u, par = 4 * pair + b, b % 2
                sp.wait_ge(hi_ready, 4 * u + 2)
                sp.dma_start(k_stack[0:DH, par, :, :].bitcast(F32), k_ones[0:DH, par, :, :].bitcast(F32))\
                  .then_inc(copied[par], 16)
                sp.wait_ge(hi_ready, 4 * u + 4)
                sp.dma_start(q_stack[DH:P, par, :, :].bitcast(F32), q_stack[0:DH, par, :, :].bitcast(F32))\
                  .then_inc(copied[par], 16)

            def unit(pair, b, first, left):
                if left:
                    move_max(*following(pair, b))
                if left > 1:
                    copy_upper(*following(pair, b, 2))

            copy_upper(0, 0)
            move_max(0, 0)
            copy_upper(0, 1)
            walk(sp, unit)


def experts_phase(nc, sb, sem, psum, ident, ones, x_in, xn, xt, xt_hi, xt_lo, gb, rwt, biast, down_bias,
                  small, gate_w, up_w, down_w, outr):
    with ExitStack() as st:
        w_in = sb(st, "w_in", [P, 2, 2, F])
        w_hi = sb(st, "w_hi", [P, 2, 2, F], F32R)
        w_lo = sb(st, "w_lo", [P, 2, 2, F], F32R)
        wd = sb(st, "wd", [P, 2, NF, D])
        gated = sb(st, "gated", [P, 2, S])
        hid = sb(st, "hid", [P, 2, NF, S])
        bias_now = sb(st, "bias_now", [P, 2, 2, NF])
        y = sb(st, "y", [P, NT, D])
        logit = sb(st, "logit", [P, NT, E])
        prob = sb(st, "prob", [P, NT, E])
        rank = sb(st, "rank", [P, NT, E])
        above = sb(st, "above", [P, NT, E])
        probt = sb(st, "probt", [E, T])
        stats = sb(st, "stats2", [P, NT, 6])
        mv = sb(st, "mv2", [P, NT, 2])
        norm = sb(st, "norm", [P, NT, D])

        w_loaded = [sem(f"w_loaded{par}") for par in range(2)]
        w_parted = sem("w_parted")
        logits_ready = sem("logits_ready")
        shifted = sem("shifted")
        exp_ready = sem("exp_ready")
        route_step = sem("route_step")
        prob_ready = sem("prob_ready")
        probt_turned = sem("probt_turned")
        probt_kept = sem("probt_kept")
        bias_set = sem("bias_set")
        bias_ready = sem("bias_ready")
        bias_kept = sem("bias_kept")
        gate_ready = sem("gate_ready")
        silu_ready = sem("silu_ready")
        hid_ready = sem("hid_ready")
        down_ready = sem("down_ready")
        y_added = sem("y_added")
        base_step = sem("base_step")
        base_var = sem("base_var")
        base_root = sem("base_root")
        out_ready = sem("out_ready")
        stored = sem("stored")

        gate_bank, down_bank = 0, 4

        block = st.enter_context(nc.Block())

        def experts(eng, expert):
            with eng.Fori(0, E // 2) as twice:
                for par in range(2):
                    expert(2 * twice + par, par)

        @block.sync
        def _(sp):
            def expert(e, par):
                sp.dma_start(w_in[:, par, 0, :], gate_w[bass.ds(e, 1), :, :].rearrange("e d f -> d (e f)"))\
                  .then_inc(w_loaded[par], 16)
                sp.dma_start(w_in[:, par, 1, :], up_w[bass.ds(e, 1), :, :].rearrange("e d f -> d (e f)"))\
                  .then_inc(w_loaded[par], 16)
                sp.dma_start(wd[:, par, :, :], down_w[bass.ds(e, 1), :, :].rearrange("e (c p) d -> p (e c) d", p=P))\
                  .then_inc(w_loaded[par], 16)

            expert(0, 0)
            expert(1, 1)
            with sp.Fori(1, E // 2) as twice:
                for par in range(2):
                    e = 2 * twice + par
                    sp.wait_ge(w_parted, 2 * e - 2)
                    sp.wait_ge(down_ready, 4 * e - 4)
                    expert(e, par)
            for b in range(B):
                sp.wait_ge(out_ready, b + 1)
                sp.dma_start(outr[:, TB * b:TB * b + TB, :], norm[:, TB * b:TB * b + TB, :]).then_inc(stored, 16)
            sp.wait_ge(stored, 16 * B)

        @block.gpsimd
        def _(pool):
            def split(twice, par, first):
                e = 2 * twice + par
                pool.wait_ge(w_loaded[par], 48 * twice + 48)
                if not first:
                    pool.wait_ge(gate_ready, 8 * e - 8)
                pool.tensor_tensor(w_hi[:, par, :, :], w_in[:, par, :, :],
                                   ones[:, 0:1].unsqueeze(2).to_broadcast([P, 2, F]), ALU.mult)\
                    .then_inc(w_parted, 1)
                pool.wait_ge(w_parted, 2 * e + 1)
                pool.tensor_tensor(w_lo[:, par, :, :], w_in[:, par, :, :], w_hi[:, par, :, :].bitcast(F32),
                                   ALU.subtract).then_inc(w_parted, 1)

            split(0, 0, True)
            split(0, 1, True)
            with pool.Fori(1, E // 2) as twice:
                for par in range(2):
                    split(twice, par, False)

        @block.tensor
        def _(pe):
            for t in range(NT):
                mm = pe.matmul(psum[:, 6, E * t:E * t + E], xt[:, P * t:P * t + P], rwt[:, :], start=True, stop=True)
            mm.then_inc(logits_ready, 1)

            def gate_up(e, par, blk, c, first):
                step = 8 * e + 2 * blk + c
                if first and blk == 0:
                    pass
                else:
                    pe.wait_ge(hid_ready, step - 1)
                tok, f = slice(S * blk, S * blk + S), slice(P * c, P * c + P)
                for which in range(2):
                    o = psum[:, gate_bank + 2 * c + which, :]
                    pe.matmul(o, w_hi[:, par, which, f], xt_hi[:, tok], start=True, stop=False)
                    pe.matmul(o, w_lo[:, par, which, f], xt_hi[:, tok], start=False, stop=False)
                    mm = pe.matmul(o, w_hi[:, par, which, f], xt_lo[:, tok], start=False, stop=True)
                mm.then_inc(gate_ready, 1)

            def down(e, par, blk, first):
                n = 4 * e + blk
                pe.wait_ge(hid_ready, 2 * n + 2)
                if not (first and blk < 2):
                    pe.wait_ge(y_added, 4 * n - 4)
                for t in range(TB):
                    for c in range(NF):
                        mm = pe.matmul(psum[:, down_bank + blk % 2, P * t:P * t + P],
                                       hid[:, blk % 2, c, P * t:P * t + P], wd[:, par, c, :],
                                       start=(c == 0), stop=(c == NF - 1))
                mm.then_inc(down_ready, 1)

            def expert(e, par, first):
                pe.wait_ge(w_parted, 2 * e + 2)
                for blk in range(B):
                    for c in range(NF):
                        gate_up(e, par, blk, c, first)
                    if blk:
                        down(e, par, blk - 1, first)
                    elif not first:
                        down(e - 1, 1 - par, B - 1, False)

            expert(0, 0, True)
            pe.wait_ge(prob_ready, 1)
            for b in range(B):
                bank = 6 + b % 2
                if b >= 2:
                    pe.wait_ge(probt_kept, b - 1)
                for k in range(TB):
                    mm = pe.transpose(psum[0:E, bank, P * k:P * k + P], prob[:, TB * b + k, :], ident[:, :])
                mm.then_inc(probt_turned, 1)
            for b in range(B):
                bank = 6 + b % 2
                pe.wait_ge(probt_kept, B)
                if b >= 2:
                    pe.wait_ge(bias_kept, b - 1)
                for k in range(TB):
                    t = TB * b + k
                    mm = pe.matmul(psum[:, bank, P * k:P * k + P], probt[:, P * t:P * t + P], down_bias[:, :],
                                   start=True, stop=True)
                mm.then_inc(bias_ready, 1)
            expert(1, 1, False)
            with pe.Fori(1, E // 2) as twice:
                for par in range(2):
                    expert(2 * twice + par, par, False)
            down(E - 1, 1, B - 1, False)

        @block.scalar
        def _(act):
            act.wait_ge(base_var, 1)
            act.activation(small[:, 1, :], small[:, 0, :], ACT.Sqrt).then_inc(base_root, 1)
            act.wait_ge(shifted, 1)
            act.activation(prob[:, :, :], logit[:, :, :], ACT.Exp).then_inc(exp_ready, 1)

            def expert(e, par):
                act.wait_ge(bias_set, e + 1)
                for blk in range(B):
                    for c in range(NF):
                        step = 8 * e + 2 * blk + c
                        act.wait_ge(gate_ready, step + 1)
                        if not (isinstance(e, int) and e == 0 and blk == 0):
                            act.wait_ge(hid_ready, step - 1)
                        act.activation(gated[:, c, :], psum[:, gate_bank + 2 * c, :], ACT.Silu,
                                       bias=bias_now[:, par, 0, c:c + 1])\
                           .then_inc(silu_ready, 1)

            expert(0, 0)
            expert(1, 1)
            with act.Fori(1, E // 2) as twice:
                for par in range(2):
                    expert(2 * twice + par, par)

        @block.vector
        def _(dve):
            done = 0
            for t in range(NT):
                dve.bn_stats(stats[:, t, :], xn[:, t, :]).then_inc(base_step, 1)
            done += NT
            dve.wait_ge(base_step, done)
            for t in range(NT):
                dve.bn_aggr(mv[:, t, :], stats[:, t, :]).then_inc(base_step, 1)
            done += NT
            dve.wait_ge(base_step, done)
            dve.tensor_scalar(small[:, 0, :], mv[:, :, 1], EPS, None, ALU.add).then_inc(base_var, 1)

            lg = psum[:, 6, 0:NT * E].rearrange("p (t e) -> p t e", e=E)
            n = 0
            dve.wait_ge(logits_ready, 1)
            dve.tensor_reduce(small[:, 4, :], lg, AX.X, ALU.max).then_inc(route_step, 1)
            n += 1
            dve.wait_ge(route_step, n)
            top = small[:, 4, :].unsqueeze(2).to_broadcast([P, NT, E])
            dve.tensor_tensor(logit[:, :, :], lg, top, ALU.subtract).then_inc(shifted, 1)
            dve.wait_ge(exp_ready, 1)
            dve.tensor_reduce(small[:, 5, :], prob[:, :, :], AX.X, ALU.add).then_inc(route_step, 1)
            n += 1
            dve.wait_ge(route_step, n)
            dve.reciprocal(small[:, 6, :], small[:, 5, :]).then_inc(route_step, 1)
            n += 1
            dve.wait_ge(route_step, n)
            inv = small[:, 6, :].unsqueeze(2).to_broadcast([P, NT, E])
            dve.tensor_tensor(prob[:, :, :], prob[:, :, :], inv, ALU.mult).then_inc(route_step, 1)
            dve.memset(rank[:, :, :], 0.0).then_inc(route_step, 1)
            n += 2
            dve.wait_ge(route_step, n)
            for k in range(E):
                for lo, hi, op in ((0, k + 1, ALU.is_gt), (k + 1, E, ALU.is_ge)):
                    if hi > lo:
                        other = prob[:, :, k:k + 1].to_broadcast([P, NT, hi - lo])
                        dve.tensor_tensor(above[:, :, lo:hi], other, prob[:, :, lo:hi], op).then_inc(route_step, 1)
                        n += 1
                dve.wait_ge(route_step, n)
                dve.tensor_tensor(rank[:, :, :], rank[:, :, :], above[:, :, :], ALU.add).then_inc(route_step, 1)
                n += 1
                dve.wait_ge(route_step, n)
            dve.scalar_tensor_tensor(out=prob[:, :, :], in0=rank[:, :, :], scalar=2.0, in1=prob[:, :, :],
                                     op0=ALU.is_lt, op1=ALU.mult).then_inc(route_step, 1)
            n += 1
            dve.wait_ge(route_step, n)
            dve.tensor_reduce(small[:, 5, :], prob[:, :, :], AX.X, ALU.add).then_inc(route_step, 1)
            n += 1
            dve.wait_ge(route_step, n)
            dve.tensor_scalar(small[:, 5, :], small[:, 5, :], 1e-9, None, ALU.add).then_inc(route_step, 1)
            n += 1
            dve.wait_ge(route_step, n)
            dve.reciprocal(small[:, 6, :], small[:, 5, :]).then_inc(route_step, 1)
            n += 1
            dve.wait_ge(route_step, n)
            dve.tensor_tensor(prob[:, :, :], prob[:, :, :], inv, ALU.mult).then_inc(prob_ready, 1)

            dve.wait_ge(base_root, 1)
            done = reciprocal_root(dve, small, slice(0, NT), base_step, done)
            flat = slice(0, NT)
            for t in range(NT):
                dve.tensor_scalar(norm[:, t, :], xn[:, t, :], mv[:, t, 0:1], small[:, 2, t:t + 1],
                                  ALU.subtract, ALU.mult).then_inc(base_step, 1)
            done += NT
            dve.wait_ge(base_step, done)
            gam = gb[:, 0:1, :].to_broadcast([P, NT, D])
            bet = gb[:, 1:2, :].to_broadcast([P, NT, D])
            for a, b2, op in ((norm[:, flat, :], gam, ALU.mult), (norm[:, flat, :], bet, ALU.add),
                              (norm[:, flat, :], x_in[:, flat, :], ALU.add)):
                dve.tensor_tensor(norm[:, :, :], a, b2, op).then_inc(base_step, 1)
                done += 1
                dve.wait_ge(base_step, done)

            def set_bias(e, par):
                if not isinstance(e, int) or e:
                    dve.wait_ge(silu_ready, 8 * e)
                dve.tensor_scalar(bias_now[:, par, :, :], biast[:, :, bass.ds(NF * e, NF)], 0.0, None, ALU.add)\
                   .then_inc(bias_set, 1)
                dve.wait_ge(bias_set, e + 1)

            def multiply(e, par, blk, c):
                step = 8 * e + 2 * blk + c
                dve.wait_ge(silu_ready, step + 1)
                if not (isinstance(e, int) and e == 0 and blk < 2):
                    dve.wait_ge(down_ready, 4 * e + blk - 1)
                dve.scalar_tensor_tensor(out=hid[:, blk % 2, c, :], in0=psum[:, gate_bank + 2 * c + 1, :],
                                         scalar=bias_now[:, par, 1, c:c + 1], in1=gated[:, c, :], op0=ALU.add, op1=ALU.mult)\
                   .then_inc(hid_ready, 1)

            def add_expert(e, blk, zero=False):
                n = 4 * e + blk
                dve.wait_ge(down_ready, n + 1)
                for k in range(TB):
                    t = TB * blk + k
                    if not zero:
                        dve.wait_ge(y_added, 4 * n + k - 15)
                    dve.scalar_tensor_tensor(out=y[:, t, :], in0=psum[:, down_bank + blk % 2, P * k:P * k + P],
                                             scalar=prob[:, t, bass.ds(e, 1)], in1=y[:, t, :],
                                             op0=ALU.mult, op1=ALU.add).then_inc(y_added, 1)

            def expert(e, par, first):
                set_bias(e, par)
                for blk in range(B):
                    for c in range(NF):
                        multiply(e, par, blk, c)
                    if blk:
                        add_expert(e, blk - 1, first)
                    elif not first:
                        add_expert(e - 1, B - 1, isinstance(e, int) and e == 1)

            set_bias(0, 0)
            for blk in range(2):
                for c in range(NF):
                    multiply(0, 0, blk, c)
            dve.memset(y[:, :, :], 0.0).then_inc(base_step, 1)
            done += 1
            dve.wait_ge(base_step, done)
            add_expert(0, 0, True)
            for blk in range(2, B):
                for c in range(NF):
                    multiply(0, 0, blk, c)
                add_expert(0, blk - 1, True)
            for b in range(B):
                dve.wait_ge(probt_turned, b + 1)
                dve.tensor_copy(probt[:, S * b:S * b + S], psum[0:E, 6 + b % 2, :]).then_inc(probt_kept, 1)
            for b in range(B):
                dve.wait_ge(bias_ready, b + 1)
                part = norm[:, TB * b:TB * b + TB, :].rearrange("p t d -> p (t d)")
                dve.tensor_tensor(part, psum[:, 6 + b % 2, :], part, ALU.add).then_inc(bias_kept, 1)
            expert(1, 1, False)
            with dve.Fori(1, E // 2) as twice:
                for par in range(2):
                    expert(2 * twice + par, par, False)
            add_expert(E - 1, B - 1)
            dve.wait_ge(bias_kept, B)
            for b in range(B):
                g = slice(TB * b, TB * b + TB)
                dve.wait_ge(y_added, 4 * (4 * (E - 1) + b) + TB)
                dve.tensor_tensor(norm[:, g, :], norm[:, g, :], y[:, g, :], ALU.add).then_inc(out_ready, 1)


_INS = ['L0_attn_h', 'L0_attn_Wq', 'L0_attn_Wk', 'L0_attn_Wv', 'L0_attn_Wo', 'L0_attn_gamma', 'L0_attn_beta',
        'L0_ffn_router_w', 'L0_ffn_gate_w', 'L0_ffn_gate_b', 'L0_ffn_up_w', 'L0_ffn_up_b', 'L0_ffn_down_w',
        'L0_ffn_down_b']
_OUTS = [((4, 512, 128), 'float32')]


def kernel(**inputs):
    import numpy as _np
    import concourse.bacc as _bacc
    from concourse import mybir as _mybir
    from concourse.bass_utils import run_bass_kernel_spmd as _run

    nc = _bacc.Bacc("TRN2", target_bir_lowering=False, num_devices=1)
    arrays, args = {}, []
    for name in _INS:
        a = _np.ascontiguousarray(inputs[name])
        arrays[f"in_{name}_dram"] = a
        args.append(nc.dram_tensor(f"in_{name}_dram", a.shape, _mybir.dt.from_np(a.dtype), kind="ExternalInput").ap())
    for i, (shape, dtype) in enumerate(_OUTS):
        dt = _mybir.dt.from_np(_np.dtype(dtype))
        args.append(nc.dram_tensor(f"out_{i}_dram", shape, dt, kind="ExternalOutput").ap())
    layer_kernel(nc, *args)
    r = _run(nc, [arrays], core_ids=[0])
    got = tuple(r.results[0][f"out_{i}_dram"] for i in range(len(_OUTS)))
    return got[0]
```

```python
from contextlib import ExitStack

import concourse.bass as bass
from concourse import mybir

ALU = mybir.AluOpType
ACT = mybir.ActivationFunctionType
AX = mybir.AxisListType
F32 = mybir.dt.float32
F32R = mybir.dt.float32r

P = 128
B, S, D = 4, 512, 128
T = B * S
NT = T // P
TB = S // P
DH = 64
NP = 8
E = 8
F = 256
NF = F // P
EPS = 1e-5
SCALE = DH ** -0.5


def layer_kernel(nc: bass.Bass, x, wq, wk, wv, wo, gamma, beta, router_w,
                 gate_w, gate_b, up_w, up_b, down_w, down_b, out):
    xr = x.rearrange("b (t p) d -> p (b t) d", p=P)
    outr = out.rearrange("b (t p) d -> p (b t) d", p=P)

    with ExitStack() as ctx:
        def sb(stack, name, shape, dt=F32):
            return stack.enter_context(nc.sbuf_tensor(name, shape, dt))

        def sem(name):
            return ctx.enter_context(nc.semaphore(name))

        ident = sb(ctx, "ident", [P, P])
        ones = sb(ctx, "ones", [P, P])
        x_in = sb(ctx, "x_in", [P, NT, D])
        xn = sb(ctx, "xn", [P, NT, D])
        xt_hi = sb(ctx, "xt_hi", [P, T], F32R)
        xt_lo = sb(ctx, "xt_lo", [P, T], F32R)
        gb = sb(ctx, "gb", [P, 2, D])
        logit = sb(ctx, "logit", [P, NT, E])
        biast = sb(ctx, "biast", [P, 2, E * NF])
        down_bias = sb(ctx, "down_bias", [E, D])
        small = sb(ctx, "small", [P, 8, NT])

        psum = ctx.enter_context(nc.psum_tensor("psum", [P, 8, 512], F32))

        prepare_phase(nc, ctx, sb, sem, psum, ident, ones, x_in, xn, xt_hi, xt_lo, gb, logit, biast,
                      down_bias, small, xr, wq, wk, wv, wo, gamma, beta, router_w, gate_b, up_b, down_b)
        experts_phase(nc, sb, sem, psum, ident, ones, x_in, xn, xt_hi, xt_lo, gb, logit, biast, down_bias,
                      small, gate_w, up_w, down_w, outr)


def prepare_phase(nc, ctx, sb, sem, psum, ident, ones, x_in, xn, xt_hi, xt_lo, gb, logit, biast,
                  down_bias, small, xr, wq, wk, wv, wo, gamma, beta, router_w, gate_b, up_b, down_b):
    with ExitStack() as att:
        wqk = sb(att, "wqk", [P, 2, NP * P])
        wo_sb = sb(att, "wo_sb", [P, NP, D])
        v_all = sb(att, "v_all", [P, NT, NP * P])
        wqk_hi = sb(att, "wqk_hi", [P, 2, P], F32R)
        wqk_lo = sb(att, "wqk_lo", [P, 2, P], F32R)

        x_loaded = [sem(f"x_loaded{b}") for b in range(B)]
        wv_loaded = sem("wv_loaded")
        rows_loaded = sem("rows_loaded")
        weights_loaded = sem("weights_loaded")
        const_made = sem("const_made")
        wv_split = sem("wv_split")
        stat_step = sem("stat_step")
        var_ready = sem("var_ready")
        root_ready = sem("root_ready")
        xn_ready = sem("xn_ready")
        xt_turned = sem("xt_turned")
        xt_copied = sem("xt_copied")
        xt_hi_ready = sem("xt_hi_ready")
        xt_lo_ready = sem("xt_lo_ready")
        rows_turned = sem("rows_turned")
        rows_kept = sem("rows_kept")
        logits_ready = sem("logits_ready")
        logits_kept = sem("logits_kept")
        v_ready = sem("v_ready")
        v_kept_act = sem("v_kept_act")
        v_kept_dve = sem("v_kept_dve")
        w_split = sem("w_split")

        with ExitStack() as prep:
            xt = sb(prep, "xt", [P, T])
            rwt = sb(prep, "rwt", [P, E])
            wv_in = sb(prep, "wv_in", [P, NP * P])
            wv_hi = sb(prep, "wv_hi", [P, NP * P], F32R)
            wv_lo = sb(prep, "wv_lo", [P, NP * P], F32R)
            rows = sb(prep, "rows", [P, 3, D])
            grow = sb(prep, "grow", [1, 2, D])
            stats = sb(prep, "stats", [P, NT, 6])
            mv = sb(prep, "mv", [P, NT, 2])
            block = prep.enter_context(nc.Block())
            bank_x, bank_v = 0, 4
            bias_rows, router_rows = rows[0:2 * E * NF, 0, :], rows[0:E, 1, :]

            @block.sync
            def _(sp):
                for b in range(B):
                    sp.dma_start(x_in[:, TB * b:TB * b + TB, :], xr[:, TB * b:TB * b + TB, :])\
                      .then_inc(x_loaded[b], 16)
                sp.dma_start(wv_in[:, :], wv).then_inc(wv_loaded, 16)
                sp.dma_start(wqk[:, 0, :], wq).then_inc(weights_loaded, 16)
                sp.dma_start(wqk[:, 1, :], wk).then_inc(weights_loaded, 16)
                sp.dma_start(wo_sb[:, :, :], wo.rearrange("(n f) d -> f n d", f=P)).then_inc(weights_loaded, 16)

            @block.gpsimd
            def _(pool):
                pool.memset(ident[:, :], 0.0).then_inc(const_made, 1)
                pool.memset(ones[:, :], 1.0).then_inc(const_made, 1)
                pool.wait_ge(const_made, 2)
                pool.affine_select(out=ident[:, :], in_=ident[:, :], compare_op=ALU.not_equal, fill=1.0,
                                   base=0, pattern=[[-1, P]], channel_multiplier=1).then_inc(const_made, 1)
                pool.wait_ge(wv_loaded, 16)
                pool.tensor_copy(wv_hi[:, :], wv_in[:, :]).then_inc(wv_split, 1)
                pool.wait_ge(wv_split, 1)
                pool.tensor_tensor(wv_lo[:, :], wv_in[:, :], wv_hi[:, :].bitcast(F32), ALU.subtract)\
                    .then_inc(wv_split, 1)

            @block.scalar
            def _(act):
                act.dma_start(rows[0:E * NF, 0, :], gate_b.rearrange("e (c p) -> (e c) p", p=P))\
                   .then_inc(rows_loaded, 16)
                act.dma_start(rows[E * NF:2 * E * NF, 0, :], up_b.rearrange("e (c p) -> (e c) p", p=P))\
                   .then_inc(rows_loaded, 16)
                act.dma_start(router_rows, router_w).then_inc(rows_loaded, 16)
                act.dma_start(grow[:, 0, :], gamma.rearrange("(a n) -> a n", a=1)).then_inc(rows_loaded, 16)
                act.dma_start(grow[:, 1, :], beta.rearrange("(a n) -> a n", a=1)).then_inc(rows_loaded, 16)
                act.dma_start(down_bias[:, :], down_b).then_inc(rows_loaded, 16)
                for b in range(B):
                    act.wait_ge(var_ready, b + 1)
                    act.activation(small[:, 1, TB * b:TB * b + TB], small[:, 0, TB * b:TB * b + TB], ACT.Sqrt)\
                       .then_inc(root_ready, 1)
                for b in range(B):
                    act.wait_ge(xt_turned, b + 1)
                    act.activation(xt_hi[:, S * b:S * b + S], psum[:, bank_x + b, :], ACT.Copy)\
                       .then_inc(xt_hi_ready, 1)
                    act.activation(xt[:, S * b:S * b + S], psum[:, bank_x + b, :], ACT.Copy)\
                       .then_inc(xt_copied, 1)
                for t in range(NT):
                    act.wait_ge(v_ready, 2 * t + 1)
                    act.activation(v_all[:, t, 0:512], psum[:, bank_v + 2 * (t % 2), :], ACT.Copy)\
                       .then_inc(v_kept_act, 1)

            @block.vector
            def _(dve):
                step = 0
                for b in range(B):
                    g = slice(TB * b, TB * b + TB)
                    dve.wait_ge(x_loaded[b], 16)
                    for t in range(TB * b, TB * b + TB):
                        dve.bn_stats(stats[:, t, :], x_in[:, t, :]).then_inc(stat_step, 1)
                    step += TB
                    dve.wait_ge(stat_step, step)
                    for t in range(TB * b, TB * b + TB):
                        dve.bn_aggr(mv[:, t, :], stats[:, t, :]).then_inc(stat_step, 1)
                    step += TB
                    dve.wait_ge(stat_step, step)
                    dve.tensor_scalar(small[:, 0, g], mv[:, g, 1], EPS, None, ALU.add).then_inc(var_ready, 1)
                for b in range(B):
                    g = slice(TB * b, TB * b + TB)
                    dve.wait_ge(root_ready, b + 1)
                    step = reciprocal_root(dve, small, g, stat_step, step)
                    for t in range(TB * b, TB * b + TB):
                        dve.tensor_scalar(xn[:, t, :], x_in[:, t, :], mv[:, t, 0:1], small[:, 2, t:t + 1],
                                          ALU.subtract, ALU.mult).then_inc(xn_ready, 1)
                dve.wait_ge(weights_loaded, 48)
                dve.tensor_copy(wqk_hi[:, :, :], wqk[:, :, 0:P]).then_inc(w_split, 1)
                dve.wait_ge(w_split, 1)
                dve.tensor_tensor(wqk_lo[:, :, :], wqk[:, :, 0:P], wqk_hi[:, :, :].bitcast(F32), ALU.subtract)\
                   .then_inc(w_split, 1)
                for b in range(B):
                    dve.wait_ge(xt_hi_ready, b + 1)
                    dve.wait_ge(xt_copied, b + 1)
                    dve.tensor_tensor(xt_lo[:, S * b:S * b + S], psum[:, bank_x + b, :],
                                      xt_hi[:, S * b:S * b + S].bitcast(F32), ALU.subtract)\
                       .then_inc(xt_lo_ready, 1)
                dve.wait_ge(rows_turned, 1)
                dve.tensor_copy(biast[:, :, :].rearrange("p a n -> p (a n)"), psum[:, bank_x, 0:2 * E * NF])\
                   .then_inc(rows_kept, 1)
                dve.tensor_copy(rwt[:, :], psum[:, bank_x, 64:64 + E]).then_inc(rows_kept, 1)
                dve.tensor_copy(gb[:, :, :].rearrange("p a n -> p (a n)"), psum[:, bank_x, 128:128 + 2 * D])\
                   .then_inc(rows_kept, 1)
                for t in range(NT):
                    dve.wait_ge(v_ready, 2 * t + 2)
                    dve.tensor_copy(v_all[:, t, 512:1024], psum[:, bank_v + 1 + 2 * (t % 2), :])\
                       .then_inc(v_kept_dve, 1)
                dve.wait_ge(logits_ready, 1)
                dve.tensor_copy(logit[:, :, :].rearrange("p t e -> p (t e)"), psum[:, bank_x, 0:NT * E])\
                   .then_inc(logits_kept, 1)

            @block.tensor
            def _(pe):
                pe.wait_ge(const_made, 3)
                for b in range(B):
                    for k in range(TB):
                        pe.wait_ge(xn_ready, TB * b + k + 1)
                        mm = pe.transpose(psum[:, bank_x + b, P * k:P * k + P], xn[:, TB * b + k, :], ident[:, :])
                    mm.then_inc(xt_turned, 1)
                pe.wait_ge(rows_loaded, 96)
                pe.wait_ge(xt_lo_ready, 1)
                n = 2 * E * NF
                pe.transpose(psum[:, bank_x, 0:n], bias_rows, ident[0:n, 0:n])
                pe.transpose(psum[:, bank_x, 64:64 + E], router_rows, ident[0:E, 0:E])
                for a in range(2):
                    mm = pe.matmul(psum[:, bank_x, 128 + D * a:128 + D * a + D], ones[0:1, :], grow[:, a, :],
                                   start=True, stop=True)
                mm.then_inc(rows_turned, 1)
                pe.wait_ge(wv_split, 2)
                for t in range(NT):
                    pe.wait_ge(xt_lo_ready, t // TB + 1)
                    for half in range(2):
                        if t >= 2:
                            pe.wait_ge((v_kept_act, v_kept_dve)[half], t - 1)
                        bank = psum[:, bank_v + half + 2 * (t % 2), :]
                        cols, tok = slice(512 * half, 512 * half + 512), slice(P * t, P * t + P)
                        pe.matmul(bank, xt_hi[:, tok], wv_hi[:, cols], start=True, stop=False)
                        pe.matmul(bank, xt_hi[:, tok], wv_lo[:, cols], start=False, stop=False)
                        pe.matmul(bank, xt_lo[:, tok], wv_hi[:, cols], start=False, stop=True).then_inc(v_ready, 1)
                pe.wait_ge(rows_kept, 3)
                for t in range(NT):
                    mm = pe.matmul(psum[:, bank_x, E * t:E * t + E], xt[:, P * t:P * t + P], rwt[:, :],
                                   start=True, stop=True)
                mm.then_inc(logits_ready, 1)

        attention_phase(nc, att, sb, sem, psum, ident, ones, xn, xt_hi, xt_lo, wqk, wo_sb, v_all,
                        wqk_hi, wqk_lo, w_split)


def reciprocal_root(dve, small, g, stat_step, step):
    dve.reciprocal(small[:, 2, g], small[:, 1, g]).then_inc(stat_step, 1)
    dve.wait_ge(stat_step, step + 1)
    dve.tensor_tensor(small[:, 3, g], small[:, 2, g], small[:, 2, g], ALU.mult).then_inc(stat_step, 1)
    dve.wait_ge(stat_step, step + 2)
    dve.tensor_tensor(small[:, 3, g], small[:, 3, g], small[:, 0, g], ALU.mult).then_inc(stat_step, 1)
    dve.wait_ge(stat_step, step + 3)
    dve.tensor_scalar(small[:, 3, g], small[:, 3, g], -0.5, 1.5, ALU.mult, ALU.add).then_inc(stat_step, 1)
    dve.wait_ge(stat_step, step + 4)
    dve.tensor_tensor(small[:, 2, g], small[:, 2, g], small[:, 3, g], ALU.mult).then_inc(stat_step, 1)
    dve.wait_ge(stat_step, step + 5)
    return step + 5


def attention_phase(nc, att, sb, sem, psum, ident, ones, xn, xt_hi, xt_lo, wqk, wo_sb, v_all,
                    wqk_hi, wqk_lo, w_split):
    k_stack = sb(att, "k_stack", [P, 2, 2, S], F32R)
    q_stack = sb(att, "q_stack", [P, 2, 2, S], F32R)
    k_ones = sb(att, "k_ones", [DH + 2, 2, 2, S], F32R)
    q_max = sb(att, "q_max", [DH + 2, 2, 2, S], F32R)
    v_pair = sb(att, "v_pair", [P, 2, TB, P])
    probs = sb(att, "probs", [P, 2, TB, 2, S])
    psums = sb(att, "psums", [P, 3, 2, S])
    o_norm = sb(att, "o_norm", [P, S])
    inv_den = sb(att, "inv_den", [P, S])
    guess = sb(att, "guess", [P, S])
    o_raw = sb(att, "o_raw", [P, 2, S])
    share = sb(att, "share", [P, S])
    q_top = sb(att, "q_top", [P, 2, 2 * TB])
    neg = sb(att, "neg", [2 * TB, 2, 2, P], F32R)

    sc_bank, mx_bank = 0, 4
    q_bank, k_bank = mx_bank, mx_bank + 1
    o_psum = psum[:, 6, :]
    den_psum = psum[:, 7, :]
    turned = psum[0:2 * TB, q_bank, 0:P]

    ones_set = sem("ones_set")
    qk_ready = sem("qk_ready")
    hi_ready = sem("hi_ready")
    copied = [sem(f"copied{par}") for par in range(2)]
    o_copied = sem("o_copied")
    lo_ready = sem("lo_ready")
    top_scores = sem("top_scores")
    top_ready = sem("top_ready")
    top_turned = sem("top_turned")
    neg_ready = sem("neg_ready")
    max_rows = sem("max_rows")
    scores_ready = sem("scores_ready")
    probs_ready = sem("probs_ready")
    v_copied = [sem(f"v_copied{par}") for par in range(2)]
    part_sums = sem("part_sums")
    sums_ready = sem("sums_ready")
    pv_done = sem("pv_done")
    den_ready = sem("den_ready")
    log_ready = sem("log_ready")
    guess_ready = sem("guess_ready")
    inv_ready = sem("inv_ready")
    o_ready = sem("o_ready")
    wo_ready = sem("wo_ready")
    share_copied = sem("share_copied")
    added = sem("added")

    LAST = NP * B - 1

    def after(pair, b, n):
        return not isinstance(pair, int) or 4 * pair + b >= n

    def walk(eng, unit):
        for b in range(B):
            unit(0, b, 2)
        with eng.Fori(1, NP - 1) as pair:
            for b in range(B):
                unit(pair, b, 2)
        for b in range(B):
            unit(NP - 1, b, min(2, B - 1 - b))

    def following(pair, b, by=1):
        return (pair, b + by) if b + by < B else (pair + 1, b + by - B)

    def preceding(pair, b, by=1):
        return (pair, b - by) if b >= by else (pair - 1, b - by + B)

    with ExitStack() as run:
        block = run.enter_context(nc.Block())

        @block.tensor
        def _(pe):
            def project(pair, b):
                u, tok = 4 * pair + b, slice(S * b, S * b + S)
                pe.wait_ge(w_split, 2 * (pair + 1))
                for which, bank in ((1, k_bank), (0, q_bank)):
                    o = psum[:, bank, :]
                    if which == 0 and after(pair, b, 2):
                        pe.wait_ge(neg_ready, 2 * u)
                    elif which == 0 and after(pair, b, 1):
                        pe.wait_ge(neg_ready, 2)
                    pe.matmul(o, wqk_hi[:, which, :], xt_hi[:, tok], start=True, stop=False)
                    pe.matmul(o, wqk_lo[:, which, :], xt_hi[:, tok], start=False, stop=False)
                    pe.matmul(o, wqk_hi[:, which, :], xt_lo[:, tok], start=False, stop=True).then_inc(qk_ready, 1)

            def scores_for_max(pair, b, js):
                u, par = 4 * pair + b, b % 2
                for j in js:
                    h, qt = j // TB, j % TB
                    if j == 0:
                        pe.wait_ge(lo_ready, 4 * u + 4)
                    if j >= 2:
                        pe.wait_ge(top_ready, 8 * u + j - 1)
                    pe.matmul(psum[:, mx_bank + j % 2, :], q_stack[0:DH, par, h, P * qt:P * qt + P],
                              k_ones[0:DH, par, h, :], start=True, stop=True).then_inc(top_scores, 1)

            def turn_max(pair, b):
                u, par = 4 * pair + b, b % 2
                pe.wait_ge(top_ready, 8 * u + 8)
                pe.transpose(turned, q_top[:, par, :], ident[:, :]).then_inc(top_turned, 1)

            def scores_stacked(u, par, kt):
                for h in range(2):
                    pe.matmul(psum[:, sc_bank + 2 * (kt % 2) + h, :], k_stack[:, par, h, P * kt:P * kt + P],
                              q_stack[:, par, h, :], start=True, stop=False)

            def scores_rest(u, par, kt):
                for h in range(2):
                    mm = pe.matmul(psum[:, sc_bank + 2 * (kt % 2) + h, :], k_ones[:, par, h, P * kt:P * kt + P],
                                   q_max[:, par, h, :], start=False, stop=True)
                mm.then_inc(scores_ready, 1)

            def values(u, par, kt):
                for h in range(2):
                    mm = pe.matmul(o_psum[DH * h:DH * h + DH, :], v_pair[:, par, kt, DH * h:DH * h + DH],
                                   probs[:, par, kt, h, :], start=(kt == 0), stop=(kt == TB - 1))
                if kt == TB - 1:
                    mm.then_inc(pv_done, 1)

            def denominators(u, u_par):
                pe.wait_ge(sums_ready, u + 1)
                for h in range(2):
                    mm = pe.matmul(den_psum[DH * h:DH * h + DH, :], ones[:, 0:DH], psums[:, u_par, h, :],
                                   start=True, stop=True)
                mm.then_inc(den_ready, 1)

            def output_share(pair, b):
                u, par = 4 * pair + b, b % 2
                pe.wait_ge(o_ready, u + 1)
                for t in range(TB):
                    mm = pe.matmul(o_psum[:, P * t:P * t + P], o_norm[:, P * t:P * t + P],
                                   wo_sb[:, pair, :], start=True, stop=True)
                mm.then_inc(wo_ready, 1)

            def unit(pair, b, left):
                u, par = 4 * pair + b, b % 2
                pe.wait_ge(copied[par], 16 * (u - par) + 32)
                scores_stacked(u, par, 0)
                scores_stacked(u, par, 1)
                pe.wait_ge(max_rows, 32 * u + 32)
                scores_rest(u, par, 0)
                scores_rest(u, par, 1)
                if after(pair, b, 1):
                    pe.wait_ge(o_copied, u)
                if after(pair, b, 2):
                    output_share(*preceding(pair, b, 2))
                if left:
                    scores_for_max(*following(pair, b), range(0, 2))
                if after(pair, b, 1):
                    denominators(u - 1, 1 - par)
                if left:
                    scores_for_max(*following(pair, b), range(2, 3))
                pe.wait_ge(probs_ready, 4 * u + 1)
                scores_stacked(u, par, 2)
                scores_rest(u, par, 2)
                if left:
                    scores_for_max(*following(pair, b), range(3, 5))
                pe.wait_ge(probs_ready, 4 * u + 2)
                scores_stacked(u, par, 3)
                scores_rest(u, par, 3)
                if left:
                    scores_for_max(*following(pair, b), range(5, 6))
                pe.wait_ge(v_copied[par], 8 * (u - par) + 16)
                if after(pair, b, 2):
                    pe.wait_ge(share_copied, u - 1)
                values(u, par, 0)
                if left:
                    scores_for_max(*following(pair, b), range(6, 8))
                values(u, par, 1)
                pe.wait_ge(probs_ready, 4 * u + 3)
                values(u, par, 2)
                if left:
                    turn_max(*following(pair, b))
                pe.wait_ge(probs_ready, 4 * u + 4)
                values(u, par, 3)
                if left > 1:
                    project(*following(pair, b, 2))

            project(0, 0)
            scores_for_max(0, 0, range(8))
            turn_max(0, 0)
            project(0, 1)
            walk(pe, unit)
            pe.wait_ge(o_copied, LAST + 1)
            output_share(NP - 1, B - 2)
            denominators(LAST, 1)
            pe.wait_ge(share_copied, LAST)
            output_share(NP - 1, B - 1)

        @block.scalar
        def _(act):
            def upper(pair, b):
                u, par = 4 * pair + b, b % 2
                act.wait_ge(qk_ready, 2 * u + 1)
                for h in range(2):
                    act.activation(k_ones[0:DH, par, h, :], psum[DH * h:DH * h + DH, k_bank, :], ACT.Copy)\
                       .then_inc(hi_ready, 1)
                act.wait_ge(qk_ready, 2 * u + 2)
                for h in range(2):
                    act.activation(q_stack[0:DH, par, h, :], psum[DH * h:DH * h + DH, q_bank, :], ACT.Copy)\
                       .then_inc(hi_ready, 1)

            def copy_output(u, par):
                act.wait_ge(pv_done, u + 1)
                act.activation(o_raw[:, par, :], o_psum, ACT.Copy).then_inc(o_copied, 1)

            def guess_inverse(u):
                act.wait_ge(den_ready, u + 1)
                act.activation(guess[:, :], den_psum, ACT.Ln).then_inc(log_ready, 1)
                act.wait_ge(log_ready, u + 1)
                act.activation(guess[:, :], guess[:, :], ACT.Exp, scale=-1.0).then_inc(guess_ready, 1)

            def copy_share(u, first):
                act.wait_ge(wo_ready, u + 1)
                if not first:
                    act.wait_ge(added, u)
                act.activation(share[:, :], o_psum, ACT.Copy).then_inc(share_copied, 1)

            def exponent(u, par, kt):
                act.wait_ge(scores_ready, 4 * u + kt + 1)
                act.activation(probs[:, par, kt, :, :], psum[:, sc_bank + 2 * (kt % 2):sc_bank + 2 * (kt % 2) + 2, :],
                               ACT.Exp, scale=SCALE).then_inc(probs_ready, 1)

            def unit(pair, b, left):
                u, par = 4 * pair + b, b % 2
                if after(pair, b, 2):
                    act.wait_ge(sums_ready, u - 1)
                exponent(u, par, 0)
                exponent(u, par, 1)
                if after(pair, b, 2):
                    copy_share(u - 2, not after(pair, b, 3))
                if after(pair, b, 1):
                    guess_inverse(u - 1)
                exponent(u, par, 2)
                exponent(u, par, 3)
                copy_output(u, par)
                if left > 1:
                    upper(*following(pair, b, 2))

            act.preload_act_table_set("natural_log_exp_and_others")
            upper(0, 0)
            upper(0, 1)
            walk(act, unit)
            copy_share(LAST - 1, False)
            guess_inverse(LAST)
            copy_share(LAST, False)

        @block.vector
        def _(dve):
            def lower(pair, b):
                u, par = 4 * pair + b, b % 2
                for h in range(2):
                    dve.wait_ge(hi_ready, 4 * u + h + 1)
                    dve.tensor_tensor(k_stack[DH:P, par, h, :], psum[DH * h:DH * h + DH, k_bank, :],
                                      k_ones[0:DH, par, h, :].bitcast(F32), ALU.subtract).then_inc(lo_ready, 1)
                for h in range(2):
                    dve.wait_ge(hi_ready, 4 * u + h + 3)
                    dve.tensor_tensor(q_max[0:DH, par, h, :], psum[DH * h:DH * h + DH, q_bank, :],
                                      q_stack[0:DH, par, h, :].bitcast(F32), ALU.subtract).then_inc(lo_ready, 1)

            def maxima(pair, b, js):
                u, par = 4 * pair + b, b % 2
                for j in js:
                    dve.wait_ge(top_scores, 8 * u + j + 1)
                    dve.tensor_reduce(q_top[:, par, j:j + 1], psum[:, mx_bank + j % 2, :], AX.X, ALU.max)\
                       .then_inc(top_ready, 1)

            def negate(pair, b):
                u, par = 4 * pair + b, b % 2
                dve.wait_ge(top_turned, u + 1)
                dve.tensor_scalar(neg[:, par, 0, :], turned, -1.0, None, ALU.mult).then_inc(neg_ready, 1)
                dve.wait_ge(neg_ready, 2 * u + 1)
                dve.scalar_tensor_tensor(out=neg[:, par, 1, :], in0=turned, scalar=-1.0,
                                         in1=neg[:, par, 0, :].bitcast(F32), op0=ALU.mult, op1=ALU.subtract)\
                   .then_inc(neg_ready, 1)

            def invert(u):
                dve.wait_ge(guess_ready, u + 1)
                dve.tensor_tensor(inv_den[:, :], den_psum, guess[:, :], ALU.mult).then_inc(inv_ready, 1)
                dve.wait_ge(inv_ready, 2 * u + 1)
                dve.scalar_tensor_tensor(out=inv_den[:, :], in0=inv_den[:, :], scalar=2.0, in1=guess[:, :],
                                         op0=ALU.subtract, op1=ALU.mult).then_inc(inv_ready, 1)

            def split_weights(pair, u):
                dve.wait_ge(qk_ready, 2 * u + 2)
                src = wqk[:, :, bass.ds(pair * P, P)]
                dve.tensor_copy(wqk_hi[:, :, :], src).then_inc(w_split, 1)
                dve.wait_ge(w_split, 2 * pair + 1)
                dve.tensor_tensor(wqk_lo[:, :, :], src, wqk_hi[:, :, :].bitcast(F32), ALU.subtract)\
                   .then_inc(w_split, 1)

            def unit(pair, b, left):
                u = 4 * pair + b
                if left:
                    maxima(*following(pair, b), range(8))
                    negate(*following(pair, b))
                if after(pair, b, 1):
                    invert(u - 1)
                if left > 1:
                    lower(*following(pair, b, 2))
                if b == 1 and not (isinstance(pair, int) and pair == NP - 1):
                    split_weights(pair + 1, u + 2)

            dve.memset(k_ones[DH:DH + 2, :, :, :].rearrange("r a h s -> r (a h s)").bitcast(F32), 1.0)\
               .then_inc(ones_set, 1)
            lower(0, 0)
            maxima(0, 0, range(8))
            dve.wait_ge(ones_set, 1)
            negate(0, 0)
            lower(0, 1)
            walk(dve, unit)
            invert(LAST)

        @block.gpsimd
        def _(pool):
            def normalise(u, par):
                pool.wait_ge(o_copied, u + 1)
                pool.wait_ge(inv_ready, 2 * u + 2)
                pool.tensor_tensor(o_norm[:, :], o_raw[:, par, :], inv_den[:, :], ALU.mult).then_inc(o_ready, 1)

            def add_share(u, b, first):
                pool.wait_ge(share_copied, u + 1)
                if not first:
                    pool.wait_ge(added, u)
                total = xn[:, TB * b:TB * b + TB, :].rearrange("p t d -> p (t d)")
                pool.tensor_tensor(total, total, share[:, :], ALU.subtract).then_inc(added, 1)

            def unit(pair, b, left):
                u, par = 4 * pair + b, b % 2
                if after(pair, b, 2):
                    add_share(u - 2, (b + 2) % B, not after(pair, b, 3))
                pool.wait_ge(probs_ready, 4 * u + 2)
                if after(pair, b, 1):
                    pool.wait_ge(sums_ready, u)
                pool.tensor_tensor(psums[:, par, :, :], probs[:, par, 0, :, :], probs[:, par, 1, :, :], ALU.add)\
                    .then_inc(part_sums, 1)
                pool.wait_ge(probs_ready, 4 * u + 4)
                pool.tensor_tensor(psums[:, 2, :, :], probs[:, par, 2, :, :], probs[:, par, 3, :, :], ALU.add)\
                    .then_inc(part_sums, 1)
                pool.wait_ge(part_sums, 2 * u + 2)
                pool.tensor_tensor(psums[:, par, :, :], psums[:, par, :, :], psums[:, 2, :, :], ALU.add)\
                    .then_inc(sums_ready, 1)
                if after(pair, b, 1):
                    normalise(u - 1, 1 - par)

            walk(pool, unit)
            add_share(LAST - 1, B - 2, False)
            normalise(LAST, 1)
            add_share(LAST, B - 1, False)

        @block.sync
        def _(sp):
            def move_max(pair, b):
                u, par = 4 * pair + b, b % 2
                for part in range(2):
                    sp.wait_ge(neg_ready, 2 * u + part + 1)
                    row = q_max[DH + part:DH + part + 1, par, :, :].rearrange("r h (t q) -> r (h t) q", q=P)
                    sp.dma_start(row.bitcast(F32), neg[:, par, part, :].bitcast(F32)).then_inc(max_rows, 16)

            def copy_upper(pair, b):
                u, par = 4 * pair + b, b % 2
                sp.wait_ge(hi_ready, 4 * u + 2)
                sp.dma_start(k_stack[0:DH, par, :, :].bitcast(F32), k_ones[0:DH, par, :, :].bitcast(F32))\
                  .then_inc(copied[par], 16)
                sp.wait_ge(hi_ready, 4 * u + 4)
                sp.dma_start(q_stack[DH:P, par, :, :].bitcast(F32), q_stack[0:DH, par, :, :].bitcast(F32))\
                  .then_inc(copied[par], 16)

            def copy_v(pair, b):
                sp.dma_start(v_pair[:, b % 2, :, :], v_all[:, TB * b:TB * b + TB, bass.ds(pair * P, P)])\
                  .then_inc(v_copied[b % 2], 16)

            def unit(pair, b, left):
                if left and after(pair, b, 1):
                    sp.wait_ge(pv_done, 4 * pair + b)
                    copy_v(*following(pair, b))
                if left:
                    move_max(*following(pair, b))
                if left > 1:
                    copy_upper(*following(pair, b, 2))

            copy_upper(0, 0)
            copy_v(0, 0)
            copy_v(0, 1)
            move_max(0, 0)
            copy_upper(0, 1)
            walk(sp, unit)


def experts_phase(nc, sb, sem, psum, ident, ones, x_in, xn, xt_hi, xt_lo, gb, logit, biast, down_bias,
                  small, gate_w, up_w, down_w, outr):
    with ExitStack() as st:
        w_in = sb(st, "w_in", [P, 2, 2, F])
        w_hi = sb(st, "w_hi", [P, 2, 2, F], F32R)
        w_lo = sb(st, "w_lo", [P, 2, 2, F], F32R)
        wd = sb(st, "wd", [P, 2, NF, D])
        gated = sb(st, "gated", [P, 2, S])
        hid = sb(st, "hid", [P, 2, NF, S])
        bias_now = sb(st, "bias_now", [P, 2, 2, NF])
        y = sb(st, "y", [P, NT, D])
        prob = sb(st, "prob", [P, NT, E])
        rank = sb(st, "rank", [P, NT, E])
        above = sb(st, "above", [P, NT, E])
        probt = sb(st, "probt", [E, T])
        stats = sb(st, "stats2", [P, NT, 6])
        mv = sb(st, "mv2", [P, NT, 2])
        norm = sb(st, "norm", [P, NT, D])

        w_loaded = [sem(f"w_loaded{par}") for par in range(2)]
        w_parted = sem("w_parted")
        shifted = sem("shifted")
        exp_ready = sem("exp_ready")
        route_step = sem("route_step")
        prob_ready = sem("prob_ready")
        probt_turned = sem("probt_turned")
        probt_kept = sem("probt_kept")
        bias_set = sem("bias_set")
        bias_ready = sem("bias_ready")
        bias_kept = sem("bias_kept")
        gate_ready = sem("gate_ready")
        silu_ready = sem("silu_ready")
        hid_ready = sem("hid_ready")
        down_ready = sem("down_ready")
        y_added = sem("y_added")
        base_step = sem("base_step")
        base_var = sem("base_var")
        base_root = sem("base_root")
        out_ready = sem("out_ready")
        stored = sem("stored")

        gate_bank, down_bank = 0, 4

        block = st.enter_context(nc.Block())

        def experts(eng, expert):
            with eng.Fori(0, E // 2) as twice:
                for par in range(2):
                    expert(2 * twice + par, par)

        @block.sync
        def _(sp):
            def expert(e, par):
                sp.dma_start(w_in[:, par, 0, :], gate_w[bass.ds(e, 1), :, :].rearrange("e d f -> d (e f)"))\
                  .then_inc(w_loaded[par], 16)
                sp.dma_start(w_in[:, par, 1, :], up_w[bass.ds(e, 1), :, :].rearrange("e d f -> d (e f)"))\
                  .then_inc(w_loaded[par], 16)
                sp.dma_start(wd[:, par, :, :], down_w[bass.ds(e, 1), :, :].rearrange("e (c p) d -> p (e c) d", p=P))\
                  .then_inc(w_loaded[par], 16)

            expert(0, 0)
            expert(1, 1)
            with sp.Fori(1, E // 2) as twice:
                for par in range(2):
                    e = 2 * twice + par
                    sp.wait_ge(w_parted, 2 * e - 2)
                    sp.wait_ge(down_ready, 4 * e - 4)
                    expert(e, par)
            for b in range(B):
                sp.wait_ge(out_ready, b + 1)
                sp.dma_start(outr[:, TB * b:TB * b + TB, :], norm[:, TB * b:TB * b + TB, :]).then_inc(stored, 16)
            sp.wait_ge(stored, 16 * B)

        @block.gpsimd
        def _(pool):
            def split(twice, par, first):
                e = 2 * twice + par
                pool.wait_ge(w_loaded[par], 48 * twice + 48)
                if not first:
                    pool.wait_ge(gate_ready, 8 * e - 8)
                pool.tensor_tensor(w_hi[:, par, :, :], w_in[:, par, :, :],
                                   ones[:, 0:1].unsqueeze(2).to_broadcast([P, 2, F]), ALU.mult)\
                    .then_inc(w_parted, 1)
                pool.wait_ge(w_parted, 2 * e + 1)
                pool.tensor_tensor(w_lo[:, par, :, :], w_in[:, par, :, :], w_hi[:, par, :, :].bitcast(F32),
                                   ALU.subtract).then_inc(w_parted, 1)

            split(0, 0, True)
            split(0, 1, True)
            with pool.Fori(1, E // 2) as twice:
                for par in range(2):
                    split(twice, par, False)

        @block.tensor
        def _(pe):
            def gate_up(e, par, blk, c, first):
                step = 8 * e + 2 * blk + c
                if first and blk == 0:
                    pass
                else:
                    pe.wait_ge(hid_ready, step - 1)
                tok, f = slice(S * blk, S * blk + S), slice(P * c, P * c + P)
                for which in range(2):
                    o = psum[:, gate_bank + 2 * c + which, :]
                    pe.matmul(o, w_hi[:, par, which, f], xt_hi[:, tok], start=True, stop=False)
                    pe.matmul(o, w_lo[:, par, which, f], xt_hi[:, tok], start=False, stop=False)
                    mm = pe.matmul(o, w_hi[:, par, which, f], xt_lo[:, tok], start=False, stop=True)
                mm.then_inc(gate_ready, 1)

            def down(e, par, blk, first):
                n = 4 * e + blk
                pe.wait_ge(hid_ready, 2 * n + 2)
                if not (first and blk < 2):
                    pe.wait_ge(y_added, 4 * n - 4)
                for t in range(TB):
                    for c in range(NF):
                        mm = pe.matmul(psum[:, down_bank + blk % 2, P * t:P * t + P],
                                       hid[:, blk % 2, c, P * t:P * t + P], wd[:, par, c, :],
                                       start=(c == 0), stop=(c == NF - 1))
                mm.then_inc(down_ready, 1)

            def expert(e, par, first):
                pe.wait_ge(w_parted, 2 * e + 2)
                for blk in range(B):
                    for c in range(NF):
                        gate_up(e, par, blk, c, first)
                    if blk:
                        down(e, par, blk - 1, first)
                    elif not first:
                        down(e - 1, 1 - par, B - 1, False)

            expert(0, 0, True)
            pe.wait_ge(prob_ready, 1)
            for b in range(B):
                bank = 6 + b % 2
                if b >= 2:
                    pe.wait_ge(probt_kept, b - 1)
                for k in range(TB):
                    mm = pe.transpose(psum[0:E, bank, P * k:P * k + P], prob[:, TB * b + k, :], ident[:, :])
                mm.then_inc(probt_turned, 1)
            for b in range(B):
                bank = 6 + b % 2
                pe.wait_ge(probt_kept, B)
                if b >= 2:
                    pe.wait_ge(bias_kept, b - 1)
                for k in range(TB):
                    t = TB * b + k
                    mm = pe.matmul(psum[:, bank, P * k:P * k + P], probt[:, P * t:P * t + P], down_bias[:, :],
                                   start=True, stop=True)
                mm.then_inc(bias_ready, 1)
            expert(1, 1, False)
            with pe.Fori(1, E // 2) as twice:
                for par in range(2):
                    expert(2 * twice + par, par, False)
            down(E - 1, 1, B - 1, False)

        @block.scalar
        def _(act):
            act.wait_ge(base_var, 1)
            act.activation(small[:, 1, :], small[:, 0, :], ACT.Sqrt).then_inc(base_root, 1)
            act.wait_ge(shifted, 1)
            act.activation(prob[:, :, :], logit[:, :, :], ACT.Exp).then_inc(exp_ready, 1)

            def expert(e, par):
                act.wait_ge(bias_set, e + 1)
                for blk in range(B):
                    for c in range(NF):
                        step = 8 * e + 2 * blk + c
                        act.wait_ge(gate_ready, step + 1)
                        if not (isinstance(e, int) and e == 0 and blk == 0):
                            act.wait_ge(hid_ready, step - 1)
                        act.activation(gated[:, c, :], psum[:, gate_bank + 2 * c, :], ACT.Silu,
                                       bias=bias_now[:, par, 0, c:c + 1])\
                           .then_inc(silu_ready, 1)

            expert(0, 0)
            expert(1, 1)
            with act.Fori(1, E // 2) as twice:
                for par in range(2):
                    expert(2 * twice + par, par)

        @block.vector
        def _(dve):
            done = 0
            for t in range(NT):
                dve.bn_stats(stats[:, t, :], xn[:, t, :]).then_inc(base_step, 1)
            done += NT
            dve.wait_ge(base_step, done)
            for t in range(NT):
                dve.bn_aggr(mv[:, t, :], stats[:, t, :]).then_inc(base_step, 1)
            done += NT
            dve.wait_ge(base_step, done)
            dve.tensor_scalar(small[:, 0, :], mv[:, :, 1], EPS, None, ALU.add).then_inc(base_var, 1)

            n = 0
            dve.tensor_reduce(small[:, 4, :], logit[:, :, :], AX.X, ALU.max).then_inc(route_step, 1)
            n += 1
            dve.wait_ge(route_step, n)
            top = small[:, 4, :].unsqueeze(2).to_broadcast([P, NT, E])
            dve.tensor_tensor(logit[:, :, :], logit[:, :, :], top, ALU.subtract).then_inc(shifted, 1)
            dve.wait_ge(exp_ready, 1)
            dve.tensor_reduce(small[:, 5, :], prob[:, :, :], AX.X, ALU.add).then_inc(route_step, 1)
            n += 1
            dve.wait_ge(route_step, n)
            dve.reciprocal(small[:, 6, :], small[:, 5, :]).then_inc(route_step, 1)
            n += 1
            dve.wait_ge(route_step, n)
            inv = small[:, 6, :].unsqueeze(2).to_broadcast([P, NT, E])
            dve.tensor_tensor(prob[:, :, :], prob[:, :, :], inv, ALU.mult).then_inc(route_step, 1)
            dve.memset(rank[:, :, :], 0.0).then_inc(route_step, 1)
            n += 2
            dve.wait_ge(route_step, n)
            for k in range(E):
                for lo, hi, op in ((0, k + 1, ALU.is_gt), (k + 1, E, ALU.is_ge)):
                    if hi > lo:
                        other = prob[:, :, k:k + 1].to_broadcast([P, NT, hi - lo])
                        dve.tensor_tensor(above[:, :, lo:hi], other, prob[:, :, lo:hi], op).then_inc(route_step, 1)
                        n += 1
                dve.wait_ge(route_step, n)
                dve.tensor_tensor(rank[:, :, :], rank[:, :, :], above[:, :, :], ALU.add).then_inc(route_step, 1)
                n += 1
                dve.wait_ge(route_step, n)
            dve.scalar_tensor_tensor(out=prob[:, :, :], in0=rank[:, :, :], scalar=2.0, in1=prob[:, :, :],
                                     op0=ALU.is_lt, op1=ALU.mult).then_inc(route_step, 1)
            n += 1
            dve.wait_ge(route_step, n)
            dve.tensor_reduce(small[:, 5, :], prob[:, :, :], AX.X, ALU.add).then_inc(route_step, 1)
            n += 1
            dve.wait_ge(route_step, n)
            dve.tensor_scalar(small[:, 5, :], small[:, 5, :], 1e-9, None, ALU.add).then_inc(route_step, 1)
            n += 1
            dve.wait_ge(route_step, n)
            dve.reciprocal(small[:, 6, :], small[:, 5, :]).then_inc(route_step, 1)
            n += 1
            dve.wait_ge(route_step, n)
            dve.tensor_tensor(prob[:, :, :], prob[:, :, :], inv, ALU.mult).then_inc(prob_ready, 1)

            dve.wait_ge(base_root, 1)
            done = reciprocal_root(dve, small, slice(0, NT), base_step, done)
            flat = slice(0, NT)
            for t in range(NT):
                dve.tensor_scalar(norm[:, t, :], xn[:, t, :], mv[:, t, 0:1], small[:, 2, t:t + 1],
                                  ALU.subtract, ALU.mult).then_inc(base_step, 1)
            done += NT
            dve.wait_ge(base_step, done)
            gam = gb[:, 0:1, :].to_broadcast([P, NT, D])
            bet = gb[:, 1:2, :].to_broadcast([P, NT, D])
            for a, b2, op in ((norm[:, flat, :], gam, ALU.mult), (norm[:, flat, :], bet, ALU.add),
                              (norm[:, flat, :], x_in[:, flat, :], ALU.add)):
                dve.tensor_tensor(norm[:, :, :], a, b2, op).then_inc(base_step, 1)
                done += 1
                dve.wait_ge(base_step, done)

            def set_bias(e, par):
                if not isinstance(e, int) or e:
                    dve.wait_ge(silu_ready, 8 * e)
                dve.tensor_scalar(bias_now[:, par, :, :], biast[:, :, bass.ds(NF * e, NF)], 0.0, None, ALU.add)\
                   .then_inc(bias_set, 1)
                dve.wait_ge(bias_set, e + 1)

            def multiply(e, par, blk, c):
                step = 8 * e + 2 * blk + c
                dve.wait_ge(silu_ready, step + 1)
                if not (isinstance(e, int) and e == 0 and blk < 2):
                    dve.wait_ge(down_ready, 4 * e + blk - 1)
                dve.scalar_tensor_tensor(out=hid[:, blk % 2, c, :], in0=psum[:, gate_bank + 2 * c + 1, :],
                                         scalar=bias_now[:, par, 1, c:c + 1], in1=gated[:, c, :], op0=ALU.add, op1=ALU.mult)\
                   .then_inc(hid_ready, 1)

            def add_expert(e, blk, zero=False):
                n = 4 * e + blk
                dve.wait_ge(down_ready, n + 1)
                for k in range(TB):
                    t = TB * blk + k
                    if not zero:
                        dve.wait_ge(y_added, 4 * n + k - 15)
                    dve.scalar_tensor_tensor(out=y[:, t, :], in0=psum[:, down_bank + blk % 2, P * k:P * k + P],
                                             scalar=prob[:, t, bass.ds(e, 1)], in1=y[:, t, :],
                                             op0=ALU.mult, op1=ALU.add).then_inc(y_added, 1)

            def expert(e, par, first):
                set_bias(e, par)
                for blk in range(B):
                    for c in range(NF):
                        multiply(e, par, blk, c)
                    if blk:
                        add_expert(e, blk - 1, first)
                    elif not first:
                        add_expert(e - 1, B - 1, isinstance(e, int) and e == 1)

            set_bias(0, 0)
            for blk in range(2):
                for c in range(NF):
                    multiply(0, 0, blk, c)
            dve.memset(y[:, :, :], 0.0).then_inc(base_step, 1)
            done += 1
            dve.wait_ge(base_step, done)
            add_expert(0, 0, True)
            for blk in range(2, B):
                for c in range(NF):
                    multiply(0, 0, blk, c)
                add_expert(0, blk - 1, True)
            for b in range(B):
                dve.wait_ge(probt_turned, b + 1)
                dve.tensor_copy(probt[:, S * b:S * b + S], psum[0:E, 6 + b % 2, :]).then_inc(probt_kept, 1)
            for b in range(B):
                dve.wait_ge(bias_ready, b + 1)
                part = norm[:, TB * b:TB * b + TB, :].rearrange("p t d -> p (t d)")
                dve.tensor_tensor(part, psum[:, 6 + b % 2, :], part, ALU.add).then_inc(bias_kept, 1)
            expert(1, 1, False)
            with dve.Fori(1, E // 2) as twice:
                for par in range(2):
                    expert(2 * twice + par, par, False)
            add_expert(E - 1, B - 1)
            dve.wait_ge(bias_kept, B)
            for b in range(B):
                g = slice(TB * b, TB * b + TB)
                dve.wait_ge(y_added, 4 * (4 * (E - 1) + b) + TB)
                dve.tensor_tensor(norm[:, g, :], norm[:, g, :], y[:, g, :], ALU.add).then_inc(out_ready, 1)


_INS = ['L0_attn_h', 'L0_attn_Wq', 'L0_attn_Wk', 'L0_attn_Wv', 'L0_attn_Wo', 'L0_attn_gamma', 'L0_attn_beta',
        'L0_ffn_router_w', 'L0_ffn_gate_w', 'L0_ffn_gate_b', 'L0_ffn_up_w', 'L0_ffn_up_b', 'L0_ffn_down_w',
        'L0_ffn_down_b']
_OUTS = [((4, 512, 128), 'float32')]


def kernel(**inputs):
    import numpy as _np
    import concourse.bacc as _bacc
    from concourse import mybir as _mybir
    from concourse.bass_utils import run_bass_kernel_spmd as _run

    nc = _bacc.Bacc("TRN2", target_bir_lowering=False, num_devices=1)
    arrays, args = {}, []
    for name in _INS:
        a = _np.ascontiguousarray(inputs[name])
        arrays[f"in_{name}_dram"] = a
        args.append(nc.dram_tensor(f"in_{name}_dram", a.shape, _mybir.dt.from_np(a.dtype), kind="ExternalInput").ap())
    for i, (shape, dtype) in enumerate(_OUTS):
        dt = _mybir.dt.from_np(_np.dtype(dtype))
        args.append(nc.dram_tensor(f"out_{i}_dram", shape, dt, kind="ExternalOutput").ap())
    layer_kernel(nc, *args)
    r = _run(nc, [arrays], core_ids=[0])
    got = tuple(r.results[0][f"out_{i}_dram"] for i in range(len(_OUTS)))
    return got[0]
```

```python
from contextlib import ExitStack

import concourse.bass as bass
from concourse import mybir

ALU = mybir.AluOpType
ACT = mybir.ActivationFunctionType
AX = mybir.AxisListType
F32 = mybir.dt.float32
F32R = mybir.dt.float32r

P = 128
B, S, D = 4, 512, 128
T = B * S
NT = T // P
TB = S // P
DH = 64
NP = 8
E = 8
F = 256
NF = F // P
EPS = 1e-5
SCALE = DH ** -0.5


def layer_kernel(nc: bass.Bass, x, wq, wk, wv, wo, gamma, beta, router_w,
                 gate_w, gate_b, up_w, up_b, down_w, down_b, out):
    xr = x.rearrange("b (t p) d -> p (b t) d", p=P)
    outr = out.rearrange("b (t p) d -> p (b t) d", p=P)

    with ExitStack() as ctx:
        def sb(name, shape, dt=F32):
            return ctx.enter_context(nc.sbuf_tensor(name, shape, dt))

        def sem(name):
            return ctx.enter_context(nc.semaphore(name))

        ident = sb("ident", [P, P])
        ones = sb("ones", [P, P])
        rest = sb("rest", [P, NT, D])
        xn = sb("xn", [P, NT, D])
        xt_hi = sb("xt_hi", [P, T], F32R)
        xt_lo = sb("xt_lo", [P, T], F32R)
        gb = sb("gb", [P, 2, D])
        prob = sb("prob", [P, NT, E])
        biast = sb("biast", [P, 2, E * NF])
        bias_now = sb("bias_now", [P, 2, 2, NF])
        down_bias = sb("down_bias", [E, D])
        small = sb("small", [P, 8, NT])
        wqk = sb("wqk", [P, 2, NP * P])
        wo_sb = sb("wo_sb", [P, NP, D])
        v_all = sb("v_all", [P, NT, NP * P])
        wqk_hi = sb("wqk_hi", [P, 2, P], F32R)
        wqk_lo = sb("wqk_lo", [P, 2, P], F32R)

        k_stack = sb("k_stack", [P, 2, 2, S], F32R)
        q_stack = sb("q_stack", [P, 2, 2, S], F32R)
        k_ones = sb("k_ones", [DH + 2, 2, 2, S], F32R)
        q_max = sb("q_max", [DH + 2, 2, 2, S], F32R)
        v_pair = sb("v_pair", [P, 2, TB, P])
        work = sb("work", [P, 2 * TB * 2 * S])
        psums = sb("psums", [P, 3, 2, S])
        o_norm = sb("o_norm", [P, S])
        inv_den = sb("inv_den", [P, S])
        guess = sb("guess", [P, S])
        o_raw = sb("o_raw", [P, 2, S])
        share = sb("share", [P, S])
        q_top = sb("q_top", [P, 2, 2 * TB])
        neg = sb("neg", [2 * TB, 2, 2, P], F32R)

        probs = work[:, :].rearrange("p (a k h s) -> p a k h s", a=2, k=TB, h=2)
        used = 0

        def take(n):
            nonlocal used
            used += n
            return work[:, used - n:used]

        xt = take(T)
        wv_in = take(NP * P)
        wv_hi = k_stack[:, 1, :, :].rearrange("p h s -> p (h s)")
        wv_lo = q_stack[:, 1, :, :].rearrange("p h s -> p (h s)")
        rows = take(2 * D).rearrange("p (a d) -> p a d", a=2)
        bias_rows, router_rows = rows[0:2 * E * NF, 0, :], rows[0:E, 1, :]
        grow = take(2 * D).rearrange("p (a d) -> p a d", a=2)[0:1, :, :]
        rwt = take(E)
        stats = take(NT * 6).rearrange("p (t s) -> p t s", s=6)
        mv = take(NT * 2).rearrange("p (t s) -> p t s", s=2)

        above = wqk[:, 0, 0:NT * E * E].rearrange("p (t e k) -> p t e k", e=E, k=E)
        rank = wqk[:, 1, 0:NT * E].rearrange("p (t e) -> p t e", e=E)

        def spare(row, n):
            return v_all[:, row, 0:n]

        w_in = [spare(4 * i, 2 * F).rearrange("p (w f) -> p w f", w=2) for i in range(2)]
        stacks = (k_stack, q_stack)
        w_hi = [stacks[i][:, 0, 0, :].rearrange("p (w f) -> p w f", w=2) for i in range(2)]
        w_lo = [stacks[i][:, 0, 1, :].rearrange("p (w f) -> p w f", w=2) for i in range(2)]
        wd = [spare(4 * i + 3, NF * D).rearrange("p (c d) -> p c d", c=NF) for i in range(2)]
        hid = [v_all[:, 8 + 2 * i:10 + 2 * i, 0:S] for i in range(2)]
        gated = [spare(12 + c, S) for c in range(NF)]
        stats2 = spare(14, NT * 6).rearrange("p (t s) -> p t s", s=6)
        probt = v_all[0:E, 14, 128:128 + S]
        mv2 = spare(15, NT * 2).rearrange("p (t s) -> p t s", s=2)

        psum = ctx.enter_context(nc.psum_tensor("psum", [P, 8, 512], F32))
        v_bank = 0
        turn_bank = 6
        sc_bank, mx_bank = 0, 4
        q_bank, k_bank = mx_bank, mx_bank + 1
        o_psum = psum[:, 6, :]
        den_psum = psum[:, 7, :]
        turned = psum[0:2 * TB, q_bank, 0:P]
        gate_bank, down_bank = 0, 4

        x_loaded = [sem(f"x_loaded{b}") for b in range(B)]
        wv_loaded = sem("wv_loaded")
        rows_loaded = sem("rows_loaded")
        weights_loaded = sem("weights_loaded")
        const_made = sem("const_made")
        wv_rounded = sem("wv_rounded")
        wv_split = sem("wv_split")
        stat_step = sem("stat_step")
        var_ready = sem("var_ready")
        root_ready = sem("root_ready")
        xn_ready = sem("xn_ready")
        xt_turned = sem("xt_turned")
        xt_hi_ready = sem("xt_hi_ready")
        xt_copied = sem("xt_copied")
        xt_lo_ready = sem("xt_lo_ready")
        rows_turned = sem("rows_turned")
        rows_kept = sem("rows_kept")
        logits_ready = sem("logits_ready")
        logits_kept = sem("logits_kept")
        v_ready = sem("v_ready")
        v_kept = sem("v_kept")
        w_split = sem("w_split")
        route_step = sem("route_step")
        shifted = sem("shifted")
        exp_ready = sem("exp_ready")
        prob_ready = sem("prob_ready")
        probt_turned = sem("probt_turned")
        probt_kept = sem("probt_kept")
        bias_ready = sem("bias_ready")
        bias_kept = sem("bias_kept")
        ones_set = sem("ones_set")
        qk_ready = sem("qk_ready")
        hi_ready = sem("hi_ready")
        copied = [sem(f"copied{par}") for par in range(2)]
        o_copied = sem("o_copied")
        lo_ready = sem("lo_ready")
        top_scores = sem("top_scores")
        top_ready = sem("top_ready")
        top_turned = sem("top_turned")
        neg_ready = sem("neg_ready")
        max_rows = sem("max_rows")
        scores_ready = sem("scores_ready")
        probs_ready = sem("probs_ready")
        v_copied = [sem(f"v_copied{par}") for par in range(2)]
        part_sums = sem("part_sums")
        sums_ready = sem("sums_ready")
        pv_done = sem("pv_done")
        den_ready = sem("den_ready")
        log_ready = sem("log_ready")
        guess_ready = sem("guess_ready")
        inv_ready = sem("inv_ready")
        o_ready = sem("o_ready")
        wo_ready = sem("wo_ready")
        share_copied = sem("share_copied")
        added = sem("added")
        w_loaded = [sem(f"w_loaded{par}") for par in range(2)]
        w_parted = sem("w_parted")
        bias_set = sem("bias_set")
        gate_ready = sem("gate_ready")
        silu_ready = sem("silu_ready")
        hid_ready = sem("hid_ready")
        down_ready = sem("down_ready")
        y_added = sem("y_added")
        base_step = sem("base_step")
        base_var = sem("base_var")
        base_root = sem("base_root")
        normed = sem("normed")
        out_ready = sem("out_ready")
        stored = sem("stored")

        LAST = NP * B - 1

        def after(pair, b, n):
            return not isinstance(pair, int) or 4 * pair + b >= n

        def walk(eng, unit, hooks=None):
            for b in range(B):
                unit(0, b, 2)
            with eng.Fori(1, NP - 1) as pair:
                for b in range(B):
                    unit(pair, b, 2)
            for b in range(B):
                if hooks and b in hooks:
                    unit(NP - 1, b, min(2, B - 1 - b), hooks[b])
                else:
                    unit(NP - 1, b, min(2, B - 1 - b))

        def following(pair, b, by=1):
            return (pair, b + by) if b + by < B else (pair + 1, b + by - B)

        def preceding(pair, b, by=1):
            return (pair, b - by) if b >= by else (pair - 1, b - by + B)

        block = ctx.enter_context(nc.Block())

        @block.tensor
        def _(pe):
            def turn(b):
                if b >= 2:
                    pe.wait_ge(xt_lo_ready, b - 1)
                for k in range(TB):
                    pe.wait_ge(xn_ready, TB * b + k + 1)
                    mm = pe.transpose(psum[:, turn_bank + b % 2, P * k:P * k + P], xn[:, TB * b + k, :], ident[:, :])
                mm.then_inc(xt_turned, 1)

            def turn_rows():
                pe.wait_ge(rows_loaded, 96)
                n = 2 * E * NF
                pe.transpose(psum[:, mx_bank, 0:n], bias_rows, ident[0:n, 0:n])
                pe.transpose(psum[:, mx_bank, 64:64 + E], router_rows, ident[0:E, 0:E])
                for a in range(2):
                    mm = pe.matmul(psum[:, mx_bank, 128 + D * a:128 + D * a + D], ones[0:1, :], grow[:, a, :],
                                   start=True, stop=True)
                mm.then_inc(rows_turned, 1)

            def project_v(tiles):
                for t in tiles:
                    pe.wait_ge(xt_lo_ready, t // TB + 1)
                    if t >= 2:
                        pe.wait_ge(v_kept, t - 1)
                    for half in range(2):
                        bank = psum[:, v_bank + half + 2 * (t % 2), :]
                        cols, tok = slice(512 * half, 512 * half + 512), slice(P * t, P * t + P)
                        pe.matmul(bank, xt_hi[:, tok], wv_hi[:, cols], start=True, stop=False)
                        pe.matmul(bank, xt_hi[:, tok], wv_lo[:, cols], start=False, stop=False)
                        mm = pe.matmul(bank, xt_lo[:, tok], wv_hi[:, cols], start=False, stop=True)
                    mm.then_inc(v_ready, 1)

            def route_logits():
                pe.wait_ge(xt_copied, B)
                pe.wait_ge(xt_lo_ready, B)
                for t in range(NT):
                    mm = pe.matmul(psum[:, turn_bank, E * t:E * t + E], xt[:, P * t:P * t + P], rwt,
                                   start=True, stop=True)
                mm.then_inc(logits_ready, 1)

            def turn_prob(b):
                if b:
                    pe.wait_ge(probt_kept, b)
                for k in range(TB):
                    mm = pe.transpose(psum[0:E, turn_bank, P * k:P * k + P], prob[:, TB * b + k, :], ident[:, :])
                mm.then_inc(probt_turned, 1)

            def routed_bias(b):
                pe.wait_ge(probt_kept, b + 1)
                if b:
                    pe.wait_ge(bias_kept, b)
                for k in range(TB):
                    mm = pe.matmul(psum[:, turn_bank + 1, P * k:P * k + P], probt[:, P * k:P * k + P],
                                   down_bias[:, :], start=True, stop=True)
                mm.then_inc(bias_ready, 1)

            def project(pair, b):
                u, tok = 4 * pair + b, slice(S * b, S * b + S)
                pe.wait_ge(w_split, 2 * (pair + 1))
                for which, bank in ((1, k_bank), (0, q_bank)):
                    o = psum[:, bank, :]
                    if which == 0 and after(pair, b, 2):
                        pe.wait_ge(neg_ready, 2 * u)
                    elif which == 0 and after(pair, b, 1):
                        pe.wait_ge(neg_ready, 2)
                    pe.matmul(o, wqk_hi[:, which, :], xt_hi[:, tok], start=True, stop=False)
                    pe.matmul(o, wqk_lo[:, which, :], xt_hi[:, tok], start=False, stop=False)
                    pe.matmul(o, wqk_hi[:, which, :], xt_lo[:, tok], start=False, stop=True).then_inc(qk_ready, 1)

            def scores_for_max(pair, b, js):
                u, par = 4 * pair + b, b % 2
                for j in js:
                    h, qt = j // TB, j % TB
                    if j == 0:
                        pe.wait_ge(lo_ready, 4 * u + 4)
                    if j >= 2:
                        pe.wait_ge(top_ready, 8 * u + j - 1)
                    pe.matmul(psum[:, mx_bank + j % 2, :], q_stack[0:DH, par, h, P * qt:P * qt + P],
                              k_ones[0:DH, par, h, :], start=True, stop=True).then_inc(top_scores, 1)

            def turn_max(pair, b):
                u, par = 4 * pair + b, b % 2
                pe.wait_ge(top_ready, 8 * u + 8)
                pe.transpose(turned, q_top[:, par, :], ident[:, :]).then_inc(top_turned, 1)

            def scores_stacked(u, par, kt):
                for h in range(2):
                    pe.matmul(psum[:, sc_bank + 2 * (kt % 2) + h, :], k_stack[:, par, h, P * kt:P * kt + P],
                              q_stack[:, par, h, :], start=True, stop=False)

            def scores_rest(u, par, kt):
                for h in range(2):
                    mm = pe.matmul(psum[:, sc_bank + 2 * (kt % 2) + h, :], k_ones[:, par, h, P * kt:P * kt + P],
                                   q_max[:, par, h, :], start=False, stop=True)
                mm.then_inc(scores_ready, 1)

            def values(u, par, kt):
                for h in range(2):
                    mm = pe.matmul(o_psum[DH * h:DH * h + DH, :], v_pair[:, par, kt, DH * h:DH * h + DH],
                                   probs[:, par, kt, h, :], start=(kt == 0), stop=(kt == TB - 1))
                if kt == TB - 1:
                    mm.then_inc(pv_done, 1)

            def denominators(u, u_par):
                pe.wait_ge(sums_ready, u + 1)
                for h in range(2):
                    mm = pe.matmul(den_psum[DH * h:DH * h + DH, :], ones[:, 0:DH], psums[:, u_par, h, :],
                                   start=True, stop=True)
                mm.then_inc(den_ready, 1)

            def last_denominators():
                pe.wait_ge(part_sums, 2 * LAST + 1)
                for h in range(2):
                    parts = (psums[:, 1, h, :], probs[:, 1, 2, h, :], probs[:, 1, 3, h, :])
                    for i, part in enumerate(parts):
                        mm = pe.matmul(den_psum[DH * h:DH * h + DH, :], ones[:, 0:DH], part,
                                       start=(i == 0), stop=(i == len(parts) - 1))
                mm.then_inc(den_ready, 1)

            def output_share(pair, b):
                u, par = 4 * pair + b, b % 2
                pe.wait_ge(o_ready, u + 1)
                for t in range(TB):
                    mm = pe.matmul(o_psum[:, P * t:P * t + P], o_norm[:, P * t:P * t + P],
                                   wo_sb[:, pair, :], start=True, stop=True)
                mm.then_inc(wo_ready, 1)

            def unit(pair, b, left):
                u, par = 4 * pair + b, b % 2
                pe.wait_ge(copied[par], 16 * (u - par) + 32)
                scores_stacked(u, par, 0)
                scores_stacked(u, par, 1)
                if after(pair, b, 2):
                    pe.wait_ge(inv_ready, 2 * u - 3)
                if after(pair, b, 1):
                    denominators(u - 1, 1 - par)
                pe.wait_ge(max_rows, 32 * u + 32)
                scores_rest(u, par, 0)
                scores_rest(u, par, 1)
                if left:
                    scores_for_max(*following(pair, b), range(0, 2))
                if after(pair, b, 1):
                    pe.wait_ge(o_copied, u)
                if after(pair, b, 2):
                    output_share(*preceding(pair, b, 2))
                if left:
                    scores_for_max(*following(pair, b), range(2, 3))
                pe.wait_ge(probs_ready, 4 * u + 1)
                scores_stacked(u, par, 2)
                scores_rest(u, par, 2)
                if left:
                    scores_for_max(*following(pair, b), range(3, 5))
                pe.wait_ge(probs_ready, 4 * u + 2)
                scores_stacked(u, par, 3)
                scores_rest(u, par, 3)
                if left:
                    scores_for_max(*following(pair, b), range(5, 6))
                pe.wait_ge(v_copied[par], 8 * (u - par) + 16)
                if after(pair, b, 2):
                    pe.wait_ge(share_copied, u - 1)
                if not after(pair, b, 1):
                    pe.wait_ge(logits_kept, 1)
                values(u, par, 0)
                if left:
                    scores_for_max(*following(pair, b), range(6, 8))
                values(u, par, 1)
                pe.wait_ge(probs_ready, 4 * u + 3)
                values(u, par, 2)
                if left:
                    turn_max(*following(pair, b))
                pe.wait_ge(probs_ready, 4 * u + 4)
                values(u, par, 3)
                if left > 1:
                    project(*following(pair, b, 2))

            def gate_up(e, par, blk, c, first):
                step = 8 * e + 2 * blk + c
                if not (first and blk == 0):
                    pe.wait_ge(hid_ready, step - 1)
                tok, f = slice(S * blk, S * blk + S), slice(P * c, P * c + P)
                for which in range(2):
                    o = psum[:, gate_bank + 2 * c + which, :]
                    pe.matmul(o, w_hi[par][:, which, f], xt_hi[:, tok], start=True, stop=False)
                    pe.matmul(o, w_lo[par][:, which, f], xt_hi[:, tok], start=False, stop=False)
                    mm = pe.matmul(o, w_hi[par][:, which, f], xt_lo[:, tok], start=False, stop=True)
                mm.then_inc(gate_ready, 1)

            def down(e, par, blk, first):
                n = 4 * e + blk
                pe.wait_ge(hid_ready, 2 * n + 2)
                if not (first and blk < 2):
                    pe.wait_ge(y_added, 4 * n - 4)
                for t in range(TB):
                    for c in range(NF):
                        mm = pe.matmul(psum[:, down_bank + blk % 2, P * t:P * t + P],
                                       hid[blk % 2][:, c, P * t:P * t + P], wd[par][:, c, :],
                                       start=(c == 0), stop=(c == NF - 1))
                mm.then_inc(down_ready, 1)

            def expert(e, par, first):
                pe.wait_ge(w_parted, 2 * e + 2)
                for blk in range(B):
                    for c in range(NF):
                        gate_up(e, par, blk, c, first)
                    if blk:
                        down(e, par, blk - 1, first)
                    elif not first:
                        down(e - 1, 1 - par, B - 1, False)

            pe.wait_ge(const_made, 3)
            turn(0)
            turn_rows()
            turn(1)
            pe.wait_ge(wv_split, 1)
            project_v(range(0, 4))
            turn(2)
            pe.wait_ge(rows_kept, 3)
            project(0, 0)
            project_v(range(4, 6))
            turn(3)
            for i in range(TB):
                project_v(range(6 + i, 7 + i))
                scores_for_max(0, 0, range(2 * i, 2 * i + 2))
            project_v(range(10, 11))
            turn_max(0, 0)
            project_v(range(11, NT))
            project(0, 1)
            route_logits()
            pe.wait_ge(v_kept, NT)
            walk(pe, unit)
            pe.wait_ge(inv_ready, 2 * LAST)
            last_denominators()
            pe.wait_ge(o_copied, LAST + 1)
            output_share(NP - 1, B - 2)
            pe.wait_ge(w_parted, 2)
            gate_up(0, 0, 0, 0, True)
            gate_up(0, 0, 0, 1, True)
            gate_up(0, 0, 1, 0, True)
            gate_up(0, 0, 1, 1, True)
            pe.wait_ge(share_copied, LAST)
            output_share(NP - 1, B - 1)
            down(0, 0, 0, True)
            for blk in range(2, B):
                for c in range(NF):
                    gate_up(0, 0, blk, c, True)
                down(0, 0, blk - 1, True)
            pe.wait_ge(w_parted, 4)
            pe.wait_ge(prob_ready, 1)
            pe.wait_ge(share_copied, LAST + 1)
            pe.wait_ge(inv_ready, 2 * LAST + 2)
            for blk in range(B):
                for c in range(NF):
                    gate_up(1, 1, blk, c, False)
                turn_prob(blk)
                down(*((1, 1, blk - 1) if blk else (0, 0, B - 1)), False)
                routed_bias(blk)
            with pe.Fori(1, E // 2) as twice:
                for par in range(2):
                    expert(2 * twice + par, par, False)
            down(E - 1, 1, B - 1, False)

        @block.scalar
        def _(act):
            def root(b):
                act.wait_ge(var_ready, b + 1)
                act.activation(small[:, 1, TB * b:TB * b + TB], small[:, 0, TB * b:TB * b + TB], ACT.Sqrt)\
                   .then_inc(root_ready, 1)

            def copy_xt(b):
                act.wait_ge(xt_turned, b + 1)
                act.activation(xt_hi[:, S * b:S * b + S], psum[:, turn_bank + b % 2, :], ACT.Copy)\
                   .then_inc(xt_hi_ready, 1)
                act.activation(xt[:, S * b:S * b + S], psum[:, turn_bank + b % 2, :], ACT.Copy)\
                   .then_inc(xt_copied, 1)

            def keep_v(tiles):
                for t in tiles:
                    act.wait_ge(v_ready, t + 1)
                    act.activation(v_all[:, t, :].rearrange("p (a n) -> p a n", a=2),
                                   psum[:, v_bank + 2 * (t % 2):v_bank + 2 * (t % 2) + 2, :], ACT.Copy)\
                       .then_inc(v_kept, 1)

            def upper(pair, b):
                u, par = 4 * pair + b, b % 2
                act.wait_ge(qk_ready, 2 * u + 1)
                for h in range(2):
                    act.activation(k_ones[0:DH, par, h, :], psum[DH * h:DH * h + DH, k_bank, :], ACT.Copy)\
                       .then_inc(hi_ready, 1)
                act.wait_ge(qk_ready, 2 * u + 2)
                for h in range(2):
                    act.activation(q_stack[0:DH, par, h, :], psum[DH * h:DH * h + DH, q_bank, :], ACT.Copy)\
                       .then_inc(hi_ready, 1)

            def copy_output(u, par):
                act.wait_ge(pv_done, u + 1)
                act.activation(o_raw[:, par, :], o_psum, ACT.Copy).then_inc(o_copied, 1)

            def guess_inverse(u):
                act.wait_ge(den_ready, u + 1)
                act.activation(guess[:, :], den_psum, ACT.Ln).then_inc(log_ready, 1)
                act.wait_ge(log_ready, u + 1)
                act.activation(guess[:, :], guess[:, :], ACT.Exp, scale=-1.0).then_inc(guess_ready, 1)

            def copy_share(u, first):
                act.wait_ge(wo_ready, u + 1)
                if not first:
                    act.wait_ge(added, u)
                act.activation(share[:, :], o_psum, ACT.Copy).then_inc(share_copied, 1)

            def exponent(u, par, kt):
                act.wait_ge(scores_ready, 4 * u + kt + 1)
                act.activation(probs[:, par, kt, :, :], psum[:, sc_bank + 2 * (kt % 2):sc_bank + 2 * (kt % 2) + 2, :],
                               ACT.Exp, scale=SCALE).then_inc(probs_ready, 1)

            def unit(pair, b, left):
                u, par = 4 * pair + b, b % 2
                if after(pair, b, 2):
                    act.wait_ge(sums_ready, u - 1)
                if not left:
                    act.wait_ge(shifted, 1)
                    act.activation(prob[:, :, :], prob[:, :, :], ACT.Exp).then_inc(exp_ready, 1)
                exponent(u, par, 0)
                exponent(u, par, 1)
                if after(pair, b, 2):
                    copy_share(u - 2, not after(pair, b, 3))
                if after(pair, b, 1):
                    guess_inverse(u - 1)
                exponent(u, par, 2)
                exponent(u, par, 3)
                copy_output(u, par)
                if left > 1:
                    upper(*following(pair, b, 2))

            def gate(e, par, blk, c):
                step = 8 * e + 2 * blk + c
                act.wait_ge(gate_ready, step + 1)
                if not (isinstance(e, int) and e == 0 and blk == 0):
                    act.wait_ge(hid_ready, step - 1)
                act.activation(gated[c], psum[:, gate_bank + 2 * c, :], ACT.Silu,
                               bias=bias_now[:, par, 0, c:c + 1]).then_inc(silu_ready, 1)

            def expert(e, par):
                act.wait_ge(bias_set, e + 1)
                for blk in range(B):
                    for c in range(NF):
                        gate(e, par, blk, c)

            act.dma_start(wv_in, wv).then_inc(wv_loaded, 16)
            act.preload_act_table_set("sqrt_and_others")
            root(0)
            root(1)
            act.wait_ge(wv_loaded, 16)
            act.activation(wv_hi, wv_in, ACT.Copy).then_inc(wv_rounded, 1)
            copy_xt(0)
            root(2)
            copy_xt(1)
            root(3)
            keep_v(range(0, 4))
            copy_xt(2)
            upper(0, 0)
            keep_v(range(4, 6))
            copy_xt(3)
            act.preload_act_table_set("natural_log_exp_and_others")
            keep_v(range(6, NT))
            upper(0, 1)
            act.wait_ge(logits_ready, 1)
            act.activation(prob[:, :, :].rearrange("p t e -> p (t e)"), psum[:, turn_bank, 0:NT * E], ACT.Copy)\
               .then_inc(logits_kept, 1)
            walk(act, unit)
            guess_inverse(LAST)
            copy_share(LAST - 1, False)
            act.wait_ge(bias_set, 1)
            for blk in range(B):
                for c in range(NF):
                    gate(0, 0, blk, c)
                if blk == 1:
                    copy_share(LAST, False)
            act.wait_ge(bias_set, 2)
            for blk in range(B):
                for c in range(NF):
                    gate(1, 1, blk, c)
                act.wait_ge(probt_turned, blk + 1)
                if blk:
                    act.wait_ge(bias_ready, blk)
                act.activation(probt, psum[0:E, turn_bank, :], ACT.Copy).then_inc(probt_kept, 1)
                if blk == 2:
                    act.wait_ge(base_var, 1)
                    act.activation(small[:, 1, :], small[:, 0, :], ACT.Sqrt).then_inc(base_root, 1)
            with act.Fori(1, E // 2) as twice:
                for par in range(2):
                    expert(2 * twice + par, par)

        @block.vector
        def _(dve):
            step = 0

            def variances(b):
                nonlocal step
                dve.wait_ge(x_loaded[b], 16)
                for t in range(TB * b, TB * b + TB):
                    dve.bn_stats(stats[:, t, :], rest[:, t, :]).then_inc(stat_step, 1)
                step += TB
                dve.wait_ge(stat_step, step)
                for t in range(TB * b, TB * b + TB):
                    dve.bn_aggr(mv[:, t, :], stats[:, t, :]).then_inc(stat_step, 1)
                step += TB
                dve.wait_ge(stat_step, step)
                g = slice(TB * b, TB * b + TB)
                dve.tensor_scalar(small[:, 0, g], mv[:, g, 1], EPS, None, ALU.add).then_inc(var_ready, 1)

            def norm(b):
                nonlocal step
                dve.wait_ge(root_ready, b + 1)
                step = reciprocal_root(dve, small, slice(TB * b, TB * b + TB), stat_step, step)
                for t in range(TB * b, TB * b + TB):
                    dve.tensor_scalar(xn[:, t, :], rest[:, t, :], mv[:, t, 0:1], small[:, 2, t:t + 1],
                                      ALU.subtract, ALU.mult).then_inc(xn_ready, 1)

            def lower_xt(b):
                dve.wait_ge(xt_hi_ready, b + 1)
                dve.wait_ge(xt_copied, b + 1)
                dve.tensor_tensor(xt_lo[:, S * b:S * b + S], psum[:, turn_bank + b % 2, :],
                                  xt_hi[:, S * b:S * b + S].bitcast(F32), ALU.subtract).then_inc(xt_lo_ready, 1)

            def keep_rows():
                dve.wait_ge(rows_turned, 1)
                dve.tensor_copy(biast[:, :, :].rearrange("p a n -> p (a n)"), psum[:, mx_bank, 0:2 * E * NF])\
                   .then_inc(rows_kept, 1)
                dve.tensor_copy(rwt, psum[:, mx_bank, 64:64 + E]).then_inc(rows_kept, 1)
                dve.tensor_copy(gb[:, :, :].rearrange("p a n -> p (a n)"), psum[:, mx_bank, 128:128 + 2 * D])\
                   .then_inc(rows_kept, 1)

            def route_shift():
                dve.wait_ge(logits_kept, 1)
                dve.tensor_reduce(small[:, 4, :], prob[:, :, :], AX.X, ALU.max).then_inc(route_step, 1)
                dve.wait_ge(route_step, 1)
                top = small[:, 4, :].unsqueeze(2).to_broadcast([P, NT, E])
                dve.tensor_tensor(prob[:, :, :], prob[:, :, :], top, ALU.subtract).then_inc(shifted, 1)

            inv = small[:, 6, :].unsqueeze(2).to_broadcast([P, NT, E])

            def route_softmax():
                dve.wait_ge(exp_ready, 1)
                dve.tensor_reduce(small[:, 5, :], prob[:, :, :], AX.X, ALU.add).then_inc(route_step, 1)
                dve.wait_ge(route_step, 2)
                dve.reciprocal(small[:, 6, :], small[:, 5, :]).then_inc(route_step, 1)
                dve.wait_ge(route_step, 3)
                dve.tensor_tensor(prob[:, :, :], prob[:, :, :], inv, ALU.mult).then_inc(route_step, 1)

            def route_compare():
                dve.wait_ge(route_step, 4)
                for k in range(E):
                    for lo, hi, op in ((0, k + 1, ALU.is_gt), (k + 1, E, ALU.is_ge)):
                        if hi > lo:
                            other = prob[:, :, k:k + 1].to_broadcast([P, NT, hi - lo])
                            dve.tensor_tensor(above[:, :, lo:hi, k], other, prob[:, :, lo:hi], op)\
                               .then_inc(route_step, 1)

            compared = 4 + 2 * E - 1

            def route_rank():
                dve.wait_ge(route_step, compared)
                dve.tensor_reduce(rank, above, AX.X, ALU.add).then_inc(route_step, 1)

            def route_weights():
                dve.wait_ge(route_step, compared + 1)
                dve.scalar_tensor_tensor(out=prob[:, :, :], in0=rank, scalar=2.0, in1=prob[:, :, :],
                                         op0=ALU.is_lt, op1=ALU.mult).then_inc(route_step, 1)
                dve.wait_ge(route_step, compared + 2)
                dve.tensor_reduce(small[:, 5, :], prob[:, :, :], AX.X, ALU.add).then_inc(route_step, 1)
                dve.wait_ge(route_step, compared + 3)
                dve.tensor_scalar(small[:, 5, :], small[:, 5, :], 1e-9, None, ALU.add).then_inc(route_step, 1)
                dve.wait_ge(route_step, compared + 4)
                dve.reciprocal(small[:, 6, :], small[:, 5, :]).then_inc(route_step, 1)
                dve.wait_ge(route_step, compared + 5)
                dve.tensor_tensor(prob[:, :, :], prob[:, :, :], inv, ALU.mult).then_inc(prob_ready, 1)

            def add_routed_bias(b):
                dve.wait_ge(bias_ready, b + 1)
                dve.wait_ge(y_added, TB * b + TB)
                part = rest[:, TB * b:TB * b + TB, :].rearrange("p t d -> p (t d)")
                dve.tensor_tensor(part, psum[:, turn_bank + 1, :], part, ALU.add).then_inc(bias_kept, 1)

            def lower(pair, b):
                u, par = 4 * pair + b, b % 2
                for h in range(2):
                    dve.wait_ge(hi_ready, 4 * u + h + 1)
                    dve.tensor_tensor(k_stack[DH:P, par, h, :], psum[DH * h:DH * h + DH, k_bank, :],
                                      k_ones[0:DH, par, h, :].bitcast(F32), ALU.subtract).then_inc(lo_ready, 1)
                for h in range(2):
                    dve.wait_ge(hi_ready, 4 * u + h + 3)
                    dve.tensor_tensor(q_max[0:DH, par, h, :], psum[DH * h:DH * h + DH, q_bank, :],
                                      q_stack[0:DH, par, h, :].bitcast(F32), ALU.subtract).then_inc(lo_ready, 1)

            def maxima(pair, b, js):
                u, par = 4 * pair + b, b % 2
                for j in js:
                    dve.wait_ge(top_scores, 8 * u + j + 1)
                    dve.tensor_reduce(q_top[:, par, j:j + 1], psum[:, mx_bank + j % 2, :], AX.X, ALU.max)\
                       .then_inc(top_ready, 1)

            def negate(pair, b):
                u, par = 4 * pair + b, b % 2
                dve.wait_ge(top_turned, u + 1)
                dve.tensor_scalar(neg[:, par, 0, :], turned, -1.0, None, ALU.mult).then_inc(neg_ready, 1)
                dve.wait_ge(neg_ready, 2 * u + 1)
                dve.scalar_tensor_tensor(out=neg[:, par, 1, :], in0=turned, scalar=-1.0,
                                         in1=neg[:, par, 0, :].bitcast(F32), op0=ALU.mult, op1=ALU.subtract)\
                   .then_inc(neg_ready, 1)

            def invert(u):
                dve.wait_ge(guess_ready, u + 1)
                dve.tensor_tensor(inv_den[:, :], den_psum, guess[:, :], ALU.mult).then_inc(inv_ready, 1)
                dve.wait_ge(inv_ready, 2 * u + 1)
                dve.scalar_tensor_tensor(out=inv_den[:, :], in0=inv_den[:, :], scalar=2.0, in1=guess[:, :],
                                         op0=ALU.subtract, op1=ALU.mult).then_inc(inv_ready, 1)

            def split_weights(pair, u):
                dve.wait_ge(qk_ready, 2 * u + 2)
                src = wqk[:, :, bass.ds(pair * P, P)]
                dve.tensor_copy(wqk_hi[:, :, :], src).then_inc(w_split, 1)
                dve.wait_ge(w_split, 2 * pair + 1)
                dve.tensor_tensor(wqk_lo[:, :, :], src, wqk_hi[:, :, :].bitcast(F32), ALU.subtract)\
                   .then_inc(w_split, 1)

            def unit(pair, b, left):
                u = 4 * pair + b
                if left:
                    maxima(*following(pair, b), range(8))
                    negate(*following(pair, b))
                else:
                    route_shift()
                    route_softmax()
                    route_compare()
                if after(pair, b, 1):
                    invert(u - 1)
                if not left:
                    route_rank()
                    route_weights()
                if left > 1:
                    lower(*following(pair, b, 2))
                if b == 1 and not (isinstance(pair, int) and pair == NP - 1):
                    split_weights(pair + 1, u + 2)

            def set_bias(e, par):
                if not isinstance(e, int) or e:
                    dve.wait_ge(silu_ready, 8 * e)
                dve.tensor_scalar(bias_now[:, par, :, :], biast[:, :, bass.ds(NF * e, NF)], 0.0, None, ALU.add)\
                   .then_inc(bias_set, 1)
                dve.wait_ge(bias_set, e + 1)

            def multiply(e, par, blk, c):
                step = 8 * e + 2 * blk + c
                dve.wait_ge(silu_ready, step + 1)
                if not (isinstance(e, int) and e == 0 and blk < 2):
                    dve.wait_ge(down_ready, 4 * e + blk - 1)
                dve.scalar_tensor_tensor(out=hid[blk % 2][:, c, :], in0=psum[:, gate_bank + 2 * c + 1, :],
                                         scalar=bias_now[:, par, 1, c:c + 1], in1=gated[c], op0=ALU.add, op1=ALU.mult)\
                   .then_inc(hid_ready, 1)

            def add_expert(e, blk, first=False):
                n = 4 * e + blk
                dve.wait_ge(down_ready, n + 1)
                if isinstance(e, int) and e == 1:
                    dve.wait_ge(bias_kept, blk + 1)
                for k in range(TB):
                    t = TB * blk + k
                    if not first:
                        dve.wait_ge(y_added, 4 * n + k - 15)
                    dve.scalar_tensor_tensor(out=rest[:, t, :], in0=psum[:, down_bank + blk % 2, P * k:P * k + P],
                                             scalar=prob[:, t, bass.ds(e, 1)], in1=rest[:, t, :],
                                             op0=ALU.mult, op1=ALU.add).then_inc(y_added, 1)

            def expert(e, par, between=None):
                set_bias(e, par)
                for blk in range(B):
                    for c in range(NF):
                        multiply(e, par, blk, c)
                    if blk:
                        add_expert(e, blk - 1, isinstance(e, int) and e == 0)
                    else:
                        add_expert(e - 1, B - 1, isinstance(e, int) and e == 1)
                    if between:
                        between(blk)

            def base_variances(b, done):
                g = slice(TB * b, TB * b + TB)
                dve.wait_ge(added, LAST - 2 + b)
                for t in range(TB * b, TB * b + TB):
                    dve.bn_stats(stats2[:, t, :], xn[:, t, :]).then_inc(base_step, 1)
                dve.wait_ge(base_step, done + TB)
                for t in range(TB * b, TB * b + TB):
                    dve.bn_aggr(mv2[:, t, :], stats2[:, t, :]).then_inc(base_step, 1)
                dve.wait_ge(base_step, done + 2 * TB)
                return done + 2 * TB

            dve.memset(k_ones[DH:DH + 2, :, :, :].rearrange("r a h s -> r (a h s)").bitcast(F32), 1.0)\
               .then_inc(ones_set, 1)
            variances(0)
            variances(1)
            norm(0)
            variances(2)
            norm(1)
            lower_xt(0)
            variances(3)
            norm(2)
            keep_rows()
            lower_xt(1)
            norm(3)
            dve.wait_ge(weights_loaded, 48)
            dve.tensor_copy(wqk_hi[:, :, :], wqk[:, :, 0:P]).then_inc(w_split, 1)
            dve.wait_ge(w_split, 1)
            dve.tensor_tensor(wqk_lo[:, :, :], wqk[:, :, 0:P], wqk_hi[:, :, :].bitcast(F32), ALU.subtract)\
               .then_inc(w_split, 1)
            lower_xt(2)
            lower(0, 0)
            lower_xt(3)
            maxima(0, 0, range(8))
            dve.wait_ge(ones_set, 1)
            negate(0, 0)
            lower(0, 1)
            walk(dve, unit)
            dve.wait_ge(prob_ready, 1)
            set_bias(0, 0)
            dve.wait_ge(o_ready, LAST)
            invert(LAST)
            done = 0
            for blk in range(B):
                for c in range(NF):
                    multiply(0, 0, blk, c)
                if blk:
                    add_expert(0, blk - 1, True)
                if blk >= 2:
                    done = base_variances(blk - 2, done)

            def between(blk):
                nonlocal done
                add_routed_bias(blk)
                if blk < 2:
                    done = base_variances(blk + 2, done)
                if blk == 1:
                    dve.tensor_scalar(small[:, 0, :], mv2[:, :, 1], EPS, None, ALU.add).then_inc(base_var, 1)
                if blk == 3:
                    dve.wait_ge(base_root, 1)
                    done = reciprocal_root(dve, small, slice(0, NT), base_step, done)

            expert(1, 1, between)
            with dve.Fori(1, E // 2) as twice:
                for par in range(2):
                    expert(2 * twice + par, par)
            dve.wait_ge(normed, 4)
            for b in range(B):
                if b == B - 1:
                    add_expert(E - 1, b)
                g = slice(TB * b, TB * b + TB)
                dve.wait_ge(y_added, 4 * (4 * (E - 1) + b) + TB)
                dve.tensor_tensor(xn[:, g, :], xn[:, g, :], rest[:, g, :], ALU.add).then_inc(out_ready, 1)

        @block.gpsimd
        def _(pool):
            def normalise(u, par):
                pool.wait_ge(o_copied, u + 1)
                pool.wait_ge(inv_ready, 2 * u + 2)
                pool.tensor_tensor(o_norm[:, :], o_raw[:, par, :], inv_den[:, :], ALU.mult).then_inc(o_ready, 1)

            def add_share(u, b, first):
                pool.wait_ge(share_copied, u + 1)
                if not first:
                    pool.wait_ge(added, u)
                total = xn[:, TB * b:TB * b + TB, :].rearrange("p t d -> p (t d)")
                pool.tensor_tensor(total, total, share[:, :], ALU.subtract).then_inc(added, 1)

            def unit(pair, b, left, hook=None):
                u, par = 4 * pair + b, b % 2
                if hook:
                    hook()
                pool.wait_ge(probs_ready, 4 * u + 2)
                if after(pair, b, 1):
                    pool.wait_ge(sums_ready, u)
                pool.tensor_tensor(psums[:, par, :, :], probs[:, par, 0, :, :], probs[:, par, 1, :, :], ALU.add)\
                    .then_inc(part_sums, 1)
                if after(pair, b, 2):
                    add_share(u - 2, (b + 2) % B, not after(pair, b, 3))
                if left:
                    pool.wait_ge(probs_ready, 4 * u + 4)
                    pool.tensor_tensor(psums[:, 2, :, :], probs[:, par, 2, :, :], probs[:, par, 3, :, :], ALU.add)\
                        .then_inc(part_sums, 1)
                    pool.wait_ge(part_sums, 2 * u + 2)
                    pool.tensor_tensor(psums[:, par, :, :], psums[:, par, :, :], psums[:, 2, :, :], ALU.add)\
                        .then_inc(sums_ready, 1)
                if after(pair, b, 1):
                    normalise(u - 1, 1 - par)

            def split(twice, par, first):
                e = 2 * twice + par
                pool.wait_ge(w_loaded[par], 48 * twice + 48)
                if not first:
                    pool.wait_ge(gate_ready, 8 * e - 8)
                pool.tensor_tensor(w_hi[par], w_in[par], ones[:, 0:1].unsqueeze(2).to_broadcast([P, 2, F]), ALU.mult)\
                    .then_inc(w_parted, 1)
                pool.wait_ge(w_parted, 2 * e + 1)
                pool.tensor_tensor(w_lo[par], w_in[par], w_hi[par].bitcast(F32), ALU.subtract).then_inc(w_parted, 1)

            def split_first():
                pool.wait_ge(scores_ready, 4 * LAST)
                split(0, 0, True)

            pool.memset(ident[:, :], 0.0).then_inc(const_made, 1)
            pool.memset(ones[:, :], 1.0).then_inc(const_made, 1)
            pool.wait_ge(const_made, 2)
            pool.affine_select(out=ident[:, :], in_=ident[:, :], compare_op=ALU.not_equal, fill=1.0,
                               base=0, pattern=[[-1, P]], channel_multiplier=1).then_inc(const_made, 1)
            pool.wait_ge(wv_rounded, 1)
            pool.tensor_tensor(wv_lo, wv_in, wv_hi.bitcast(F32), ALU.subtract).then_inc(wv_split, 1)
            walk(pool, unit, {B - 1: split_first})
            add_share(LAST - 1, B - 2, False)
            normalise(LAST, 1)
            add_share(LAST, B - 1, False)
            split(0, 1, True)
            with pool.Fori(1, E // 2) as twice:
                for par in range(2):
                    split(twice, par, False)
            pool.wait_ge(base_step, 2 * NT + 5)
            for n, (by, op) in enumerate(((mv2[:, :, 0:1], ALU.subtract), (small[:, 2, :].unsqueeze(2), ALU.mult),
                                          (gb[:, 0:1, :], ALU.mult), (gb[:, 1:2, :], ALU.add))):
                if n:
                    pool.wait_ge(normed, n)
                pool.tensor_tensor(xn[:, :, :], xn[:, :, :], by.to_broadcast([P, NT, D]), op).then_inc(normed, 1)

        @block.sync
        def _(sp):
            def move_max(pair, b):
                u, par = 4 * pair + b, b % 2
                for part in range(2):
                    sp.wait_ge(neg_ready, 2 * u + part + 1)
                    row = q_max[DH + part:DH + part + 1, par, :, :].rearrange("r h (t q) -> r (h t) q", q=P)
                    sp.dma_start(row.bitcast(F32), neg[:, par, part, :].bitcast(F32)).then_inc(max_rows, 16)

            def copy_upper(pair, b):
                u, par = 4 * pair + b, b % 2
                sp.wait_ge(hi_ready, 4 * u + 2)
                sp.dma_start(k_stack[0:DH, par, :, :].bitcast(F32), k_ones[0:DH, par, :, :].bitcast(F32))\
                  .then_inc(copied[par], 16)
                sp.wait_ge(hi_ready, 4 * u + 4)
                sp.dma_start(q_stack[DH:P, par, :, :].bitcast(F32), q_stack[0:DH, par, :, :].bitcast(F32))\
                  .then_inc(copied[par], 16)

            def copy_v(pair, b):
                sp.dma_start(v_pair[:, b % 2, :, :], v_all[:, TB * b:TB * b + TB, bass.ds(pair * P, P)])\
                  .then_inc(v_copied[b % 2], 16)

            def unit(pair, b, left, hook=None):
                if left and after(pair, b, 1):
                    sp.wait_ge(pv_done, 4 * pair + b)
                    copy_v(*following(pair, b))
                if left:
                    move_max(*following(pair, b))
                if left > 1:
                    copy_upper(*following(pair, b, 2))
                if hook:
                    hook()

            def load_expert(e, par):
                sp.dma_start(w_in[par][:, 0, :], gate_w[bass.ds(e, 1), :, :].rearrange("e d f -> d (e f)"))\
                  .then_inc(w_loaded[par], 16)
                sp.dma_start(w_in[par][:, 1, :], up_w[bass.ds(e, 1), :, :].rearrange("e d f -> d (e f)"))\
                  .then_inc(w_loaded[par], 16)
                sp.dma_start(wd[par], down_w[bass.ds(e, 1), :, :].rearrange("e (c p) d -> p (e c) d", p=P))\
                  .then_inc(w_loaded[par], 16)

            def load_first():
                sp.wait_ge(v_copied[0], 8 * (LAST - 5) + 16)
                sp.wait_ge(v_copied[1], 8 * (LAST - 5) + 16)
                load_expert(0, 0)
                load_expert(1, 1)

            for b in range(B):
                sp.dma_start(rest[:, TB * b:TB * b + TB, :], xr[:, TB * b:TB * b + TB, :])\
                  .then_inc(x_loaded[b], 16)
            sp.dma_start(rows[0:E * NF, 0, :], gate_b.rearrange("e (c p) -> (e c) p", p=P))\
              .then_inc(rows_loaded, 16)
            sp.dma_start(rows[E * NF:2 * E * NF, 0, :], up_b.rearrange("e (c p) -> (e c) p", p=P))\
              .then_inc(rows_loaded, 16)
            sp.dma_start(router_rows, router_w).then_inc(rows_loaded, 16)
            sp.dma_start(grow[:, 0, :], gamma.rearrange("(a n) -> a n", a=1)).then_inc(rows_loaded, 16)
            sp.dma_start(grow[:, 1, :], beta.rearrange("(a n) -> a n", a=1)).then_inc(rows_loaded, 16)
            sp.dma_start(down_bias[:, :], down_b).then_inc(rows_loaded, 16)
            sp.dma_start(wqk[:, 0, :], wq).then_inc(weights_loaded, 16)
            sp.dma_start(wqk[:, 1, :], wk).then_inc(weights_loaded, 16)
            sp.dma_start(wo_sb[:, :, :], wo.rearrange("(n f) d -> f n d", f=P)).then_inc(weights_loaded, 16)
            copy_upper(0, 0)
            sp.wait_ge(v_kept, TB)
            copy_v(0, 0)
            move_max(0, 0)
            sp.wait_ge(v_kept, 2 * TB)
            copy_v(0, 1)
            copy_upper(0, 1)
            sp.wait_ge(v_kept, NT)
            walk(sp, unit, {0: load_first})
            with sp.Fori(1, E // 2) as twice:
                for par in range(2):
                    e = 2 * twice + par
                    sp.wait_ge(w_parted, 2 * e - 2)
                    sp.wait_ge(down_ready, 4 * e - 4)
                    load_expert(e, par)
            for b in range(B):
                sp.wait_ge(out_ready, b + 1)
                sp.dma_start(outr[:, TB * b:TB * b + TB, :], xn[:, TB * b:TB * b + TB, :]).then_inc(stored, 16)
            sp.wait_ge(stored, 16 * B)


def reciprocal_root(dve, small, g, stat_step, step):
    dve.reciprocal(small[:, 2, g], small[:, 1, g]).then_inc(stat_step, 1)
    dve.wait_ge(stat_step, step + 1)
    dve.tensor_tensor(small[:, 3, g], small[:, 2, g], small[:, 2, g], ALU.mult).then_inc(stat_step, 1)
    dve.wait_ge(stat_step, step + 2)
    dve.tensor_tensor(small[:, 3, g], small[:, 3, g], small[:, 0, g], ALU.mult).then_inc(stat_step, 1)
    dve.wait_ge(stat_step, step + 3)
    dve.tensor_scalar(small[:, 3, g], small[:, 3, g], -0.5, 1.5, ALU.mult, ALU.add).then_inc(stat_step, 1)
    dve.wait_ge(stat_step, step + 4)
    dve.tensor_tensor(small[:, 2, g], small[:, 2, g], small[:, 3, g], ALU.mult).then_inc(stat_step, 1)
    dve.wait_ge(stat_step, step + 5)
    return step + 5


_INS = ['L0_attn_h', 'L0_attn_Wq', 'L0_attn_Wk', 'L0_attn_Wv', 'L0_attn_Wo', 'L0_attn_gamma', 'L0_attn_beta',
        'L0_ffn_router_w', 'L0_ffn_gate_w', 'L0_ffn_gate_b', 'L0_ffn_up_w', 'L0_ffn_up_b', 'L0_ffn_down_w',
        'L0_ffn_down_b']
_OUTS = [((4, 512, 128), 'float32')]


def kernel(**inputs):
    import numpy as _np
    import concourse.bacc as _bacc
    from concourse import mybir as _mybir
    from concourse.bass_utils import run_bass_kernel_spmd as _run

    nc = _bacc.Bacc("TRN2", target_bir_lowering=False, num_devices=1)
    arrays, args = {}, []
    for name in _INS:
        a = _np.ascontiguousarray(inputs[name])
        arrays[f"in_{name}_dram"] = a
        args.append(nc.dram_tensor(f"in_{name}_dram", a.shape, _mybir.dt.from_np(a.dtype), kind="ExternalInput").ap())
    for i, (shape, dtype) in enumerate(_OUTS):
        dt = _mybir.dt.from_np(_np.dtype(dtype))
        args.append(nc.dram_tensor(f"out_{i}_dram", shape, dt, kind="ExternalOutput").ap())
    layer_kernel(nc, *args)
    r = _run(nc, [arrays], core_ids=[0])
    got = tuple(r.results[0][f"out_{i}_dram"] for i in range(len(_OUTS)))
    return got[0]
```
